# Optimizing a Trainium2 kernel written in Bass

```python
import numpy as np
import jax
import jax.numpy as jnp

def _softmax(x, axis=-1):
    return jax.nn.softmax(x, axis=axis)

def _gelu(x):
    return jax.nn.gelu(x, approximate=True)

def _silu(x):
    return jax.nn.silu(x)

def _sigmoid(x):
    return jax.nn.sigmoid(x)

def _layernorm(x, axis=-1, eps=1e-05):
    m = jnp.mean(x, axis=axis, keepdims=True)
    v = jnp.var(x, axis=axis, keepdims=True)
    return (x - m) / jnp.sqrt(v + eps)

def _scatter_add(tgt, idx, src, axis=0):
    return tgt.at[idx].add(src)

def _segment_sum(src, seg, n):
    return jax.ops.segment_sum(src, seg, n)
kernel_name = 'mk_gnn_preln_d4_gnn_r8_6197af'

def setup_inputs(seed: int=0):
    np.random.seed(seed)
    _w = jnp.asarray

    def _rec_inputs():
        import jax
        import jax.numpy as jnp
        _gk = jax.random.key(seed)
        x = -0.0005207 + 1.001 * jax.random.normal(jax.random.fold_in(_gk, 1), (512, 512), jnp.float32)
        _s = jax.random.randint(jax.random.fold_in(_gk, 2), (8192,), 0, 512, jnp.int32)
        _d = jax.random.randint(jax.random.fold_in(_gk, 3), (8192,), 0, 512, jnp.int32)
        _loop = jnp.arange(512, dtype=jnp.int32)
        src = jnp.concatenate([_s, _d, _loop])
        dst = jnp.concatenate([_d, _s, _loop])
        _o = jnp.argsort(dst, stable=True)
        src = src[_o]
        dst = dst[_o]
        edge_type_2 = jax.random.randint(jax.random.fold_in(_gk, 12), (16896,), 0, 2, jnp.int32)
        return (x, src, dst, edge_type_2)
    x, src, dst, edge_type_2 = _rec_inputs()

    def _L0_gnn_setup():
        import jax, jax.numpy as jnp
        import numpy as np
        N, E = (512, 16384)
        D_IN, D_OUT, H = (512, 512, 8)
        HEAD = D_OUT // H
        EPS = 1e-05

        def _layer_norm(x, g, b):
            m = jnp.mean(x, axis=-1, keepdims=True)
            v = jnp.mean(jnp.square(x - m), axis=-1, keepdims=True)
            return (x - m) * jax.lax.rsqrt(v + EPS) * g + b
        key = jax.random.key(seed)
        ks = jax.random.split(key, 16)
        s = 1.0 / np.sqrt(D_OUT)
        inp = {'x': jax.random.normal(ks[0], (N, D_IN), dtype=jnp.float32), 'edge_index': jax.random.randint(ks[1], (2, E), 0, N, dtype=jnp.int64), 'Wq': jax.random.normal(ks[2], (D_OUT, D_OUT), jnp.float32) * s, 'bq': jnp.zeros((D_OUT,), jnp.float32), 'Wk': jax.random.normal(ks[3], (D_OUT, D_OUT), jnp.float32) * s, 'bk': jnp.zeros((D_OUT,), jnp.float32), 'Wv': jax.random.normal(ks[4], (D_OUT, D_OUT), jnp.float32) * s, 'bv': jnp.zeros((D_OUT,), jnp.float32), 'Wo': jax.random.normal(ks[5], (D_OUT, D_OUT), jnp.float32) * s, 'bo': jnp.zeros((D_OUT,), jnp.float32), 'W1': jax.random.normal(ks[6], (D_OUT, 2 * D_OUT), jnp.float32) * s, 'b1': jnp.zeros((2 * D_OUT,), jnp.float32), 'W2': jax.random.normal(ks[7], (2 * D_OUT, D_OUT), jnp.float32) * (1.0 / np.sqrt(2 * D_OUT)), 'b2': jnp.zeros((D_OUT,), jnp.float32), 'g1': jnp.ones((D_OUT,), jnp.float32), 'be1': jnp.zeros((D_OUT,), jnp.float32), 'g2': jnp.ones((D_OUT,), jnp.float32), 'be2': jnp.zeros((D_OUT,), jnp.float32)}
        return inp
    _L0_gnn_all = _L0_gnn_setup()
    _L0_gnn_in = {k: v for k, v in _L0_gnn_all.items() if k in ('Wq', 'bq', 'Wk', 'bk', 'Wv', 'bv', 'Wo', 'bo', 'W1', 'b1', 'W2', 'b2', 'g1', 'be1', 'g2', 'be2')}
    del _L0_gnn_all

    def _L1_gnn_setup():
        import jax, jax.numpy as jnp
        import numpy as np
        N, D, E, L = (12500, 512, 400000, 2)
        BN_EPS = 1e-05

        def _prelu(x, a):
            return jnp.where(x > 0, x, a * x)
        key = jax.random.key(seed)
        ks = jax.random.split(key, 12)
        s = 1.0 / np.sqrt(D)
        return {'x': jax.random.normal(ks[0], (N, D), dtype=jnp.float32), 'edge_index': jax.random.randint(ks[1], (2, E), 0, N, dtype=jnp.int64), 'lin_W': jax.random.uniform(ks[2], (D, D), jnp.float32, -s, s), 'lin_b': jax.random.uniform(ks[3], (D,), jnp.float32, -s, s), 'lin_a': jnp.full((D,), 0.25, dtype=jnp.float32), 'conv_W1': jax.random.uniform(ks[4], (L, D, D), jnp.float32, -s, s), 'conv_b1': jax.random.uniform(ks[5], (L, D), jnp.float32, -s, s), 'conv_a': jnp.full((L,), 0.25, dtype=jnp.float32), 'conv_W2': jax.random.uniform(ks[6], (L, D, D), jnp.float32, -s, s), 'conv_b2': jax.random.uniform(ks[7], (L, D), jnp.float32, -s, s), 'bn_gamma': jnp.ones((L, D), dtype=jnp.float32), 'bn_beta': jnp.zeros((L, D), dtype=jnp.float32)}
    _L1_gnn_all = _L1_gnn_setup()
    _L1_gnn_in = {k: v for k, v in _L1_gnn_all.items() if k in ('lin_W', 'lin_b', 'lin_a', 'conv_W1', 'conv_b1', 'conv_a', 'conv_W2', 'conv_b2', 'bn_gamma', 'bn_beta')}
    del _L1_gnn_all

    def _L2_gnn_setup():
        import jax, jax.numpy as jnp
        import numpy as np
        N_NODES = 6250
        EMBED_DIM = 512
        N_EDGES = 100000
        NEG_SLOPE = 0.01
        key = jax.random.key(seed)
        k1, k2, k3 = jax.random.split(key, 3)
        X = jax.random.normal(k1, (N_NODES, EMBED_DIM), dtype=jnp.float32)
        W = jax.random.normal(k2, (EMBED_DIM, EMBED_DIM), dtype=jnp.float32) / np.sqrt(EMBED_DIM)
        b = jnp.zeros((EMBED_DIM,), dtype=jnp.float32)
        edge_index = jax.random.randint(k3, (2, N_EDGES), 0, N_NODES, dtype=jnp.int32)
        return {'X': X, 'W': W, 'b': b, 'edge_index': edge_index}
    _L2_gnn_all = _L2_gnn_setup()
    _L2_gnn_in = {k: v for k, v in _L2_gnn_all.items() if k in ('W', 'b')}
    del _L2_gnn_all

    def _L3_gnn_setup():
        import jax, jax.numpy as jnp
        import numpy as np
        NUM_RELATIONS = 2
        NUM_BASES = 30
        HIDDEN = 512
        N_NODES = 1250
        N_EDGES = 20000

        def rgcn_gate_layer(x, row, col, edge_type, basis, att, gate_w, root, bias):
            H = x.shape[1]
            w = jnp.einsum('rb,bio->rio', att, basis)
            x_j = x[col]
            msgs = []
            for r in range(NUM_RELATIONS):
                gate = jax.nn.sigmoid(x_j @ gate_w[r, :, 0])
                msgs.append(gate[:, None] * x_j @ w[r])
            msg = jnp.where((edge_type == 0)[:, None], msgs[0], msgs[1])
            agg = jax.ops.segment_sum(msg, row, num_segments=x.shape[0])
            return agg + x @ root + bias
        key = jax.random.key(seed)
        ks = jax.random.split(key, 16)
        H, R, B = (HIDDEN, NUM_RELATIONS, NUM_BASES)
        bound = 1.0 / np.sqrt(B * H)
        u = lambda k, shape: jax.random.uniform(k, shape, jnp.float32, -bound, bound)
        inp = {'x': jax.random.normal(ks[0], (N_NODES, H), jnp.float32), 'edge_index': jax.random.randint(ks[1], (2, N_EDGES), 0, N_NODES, jnp.int32), 'edge_type': jax.random.randint(ks[2], (N_EDGES,), 0, R, jnp.int32), 'basis1': u(ks[3], (B, H, H)), 'att1': u(ks[4], (R, B)), 'gate_w1': u(ks[5], (R, H, 1)), 'root1': u(ks[6], (H, H)), 'bias1': u(ks[7], (H,)), 'basis2': u(ks[8], (B, H, H)), 'att2': u(ks[9], (R, B)), 'gate_w2': u(ks[10], (R, H, 1)), 'root2': u(ks[11], (H, H)), 'bias2': u(ks[12], (H,))}
        return inp
    _L3_gnn_all = _L3_gnn_setup()
    _L3_gnn_in = {k: v for k, v in _L3_gnn_all.items() if k in ('basis1', 'att1', 'gate_w1', 'root1', 'bias1', 'basis2', 'att2', 'gate_w2', 'root2', 'bias2')}
    del _L3_gnn_all
    return {'x': x, 'src': src, 'dst': dst, 'edge_type_2': edge_type_2, 'L0_gnn_Wq': _L0_gnn_in['Wq'], 'L0_gnn_bq': _L0_gnn_in['bq'], 'L0_gnn_Wk': _L0_gnn_in['Wk'], 'L0_gnn_bk': _L0_gnn_in['bk'], 'L0_gnn_Wv': _L0_gnn_in['Wv'], 'L0_gnn_bv': _L0_gnn_in['bv'], 'L0_gnn_Wo': _L0_gnn_in['Wo'], 'L0_gnn_bo': _L0_gnn_in['bo'], 'L0_gnn_W1': _L0_gnn_in['W1'], 'L0_gnn_b1': _L0_gnn_in['b1'], 'L0_gnn_W2': _L0_gnn_in['W2'], 'L0_gnn_b2': _L0_gnn_in['b2'], 'L0_gnn_g1': _L0_gnn_in['g1'], 'L0_gnn_be1': _L0_gnn_in['be1'], 'L0_gnn_g2': _L0_gnn_in['g2'], 'L0_gnn_be2': _L0_gnn_in['be2'], 'L1_gnn_lin_W': _L1_gnn_in['lin_W'], 'L1_gnn_lin_b': _L1_gnn_in['lin_b'], 'L1_gnn_lin_a': _L1_gnn_in['lin_a'], 'L1_gnn_conv_W1': _L1_gnn_in['conv_W1'], 'L1_gnn_conv_b1': _L1_gnn_in['conv_b1'], 'L1_gnn_conv_a': _L1_gnn_in['conv_a'], 'L1_gnn_conv_W2': _L1_gnn_in['conv_W2'], 'L1_gnn_conv_b2': _L1_gnn_in['conv_b2'], 'L1_gnn_bn_gamma': _L1_gnn_in['bn_gamma'], 'L1_gnn_bn_beta': _L1_gnn_in['bn_beta'], 'L2_gnn_W': _L2_gnn_in['W'], 'L2_gnn_b': _L2_gnn_in['b'], 'L3_gnn_basis1': _L3_gnn_in['basis1'], 'L3_gnn_att1': _L3_gnn_in['att1'], 'L3_gnn_gate_w1': _L3_gnn_in['gate_w1'], 'L3_gnn_root1': _L3_gnn_in['root1'], 'L3_gnn_bias1': _L3_gnn_in['bias1'], 'L3_gnn_basis2': _L3_gnn_in['basis2'], 'L3_gnn_att2': _L3_gnn_in['att2'], 'L3_gnn_gate_w2': _L3_gnn_in['gate_w2'], 'L3_gnn_root2': _L3_gnn_in['root2'], 'L3_gnn_bias2': _L3_gnn_in['bias2']}

def reference(x, src, dst, edge_type_2, L0_gnn_Wq, L0_gnn_bq, L0_gnn_Wk, L0_gnn_bk, L0_gnn_Wv, L0_gnn_bv, L0_gnn_Wo, L0_gnn_bo, L0_gnn_W1, L0_gnn_b1, L0_gnn_W2, L0_gnn_b2, L0_gnn_g1, L0_gnn_be1, L0_gnn_g2, L0_gnn_be2, L1_gnn_lin_W, L1_gnn_lin_b, L1_gnn_lin_a, L1_gnn_conv_W1, L1_gnn_conv_b1, L1_gnn_conv_a, L1_gnn_conv_W2, L1_gnn_conv_b2, L1_gnn_bn_gamma, L1_gnn_bn_beta, L2_gnn_W, L2_gnn_b, L3_gnn_basis1, L3_gnn_att1, L3_gnn_gate_w1, L3_gnn_root1, L3_gnn_bias1, L3_gnn_basis2, L3_gnn_att2, L3_gnn_gate_w2, L3_gnn_root2, L3_gnn_bias2):
    import jax
    import jax.numpy as jnp

    def _L0_gnn_ref(x, edge_index, Wq, bq, Wk, bk, Wv, bv, Wo, bo, W1, b1, W2, b2, g1, be1, g2, be2):
        import jax, jax.numpy as jnp
        import numpy as np
        N, E = (512, 16384)
        D_IN, D_OUT, H = (512, 512, 8)
        HEAD = D_OUT // H
        EPS = 1e-05

        def _layer_norm(x, g, b):
            m = jnp.mean(x, axis=-1, keepdims=True)
            v = jnp.mean(jnp.square(x - m), axis=-1, keepdims=True)
            return (x - m) * jax.lax.rsqrt(v + EPS) * g + b
        q = (x @ Wq + bq).reshape(N, H, HEAD)
        k = (x @ Wk + bk).reshape(N, H, HEAD)
        v = (x @ Wv + bv).reshape(N, H, HEAD)
        scores = jnp.einsum('nhd,mhd->nhm', q, k) / np.sqrt(HEAD)
        adj = jnp.zeros((N, N), jnp.float32).at[edge_index[0], edge_index[1]].set(1.0)
        scores = jnp.where(adj[:, None, :] == 0, -1000000000.0, scores)
        attn = jax.nn.softmax(scores, axis=1)
        attn_out = jnp.einsum('nhm,mhd->nhd', attn, v).reshape(N, D_OUT)
        attn_out = attn_out @ Wo + bo
        h1 = _layer_norm(x + attn_out, g1, be1)
        ff = jax.nn.relu(h1 @ W1 + b1) @ W2 + b2
        return _layer_norm(h1 + ff, g2, be2)

    def _L1_gnn_ref(x, edge_index, lin_W, lin_b, lin_a, conv_W1, conv_b1, conv_a, conv_W2, conv_b2, bn_gamma, bn_beta):
        import jax, jax.numpy as jnp
        import numpy as np
        N, D, E, L = (12500, 512, 400000, 2)
        BN_EPS = 1e-05

        def _prelu(x, a):
            return jnp.where(x > 0, x, a * x)
        n = x.shape[0]
        src, dst = (edge_index[0], edge_index[1])
        x = _prelu(x @ lin_W.T + lin_b, lin_a)
        for l in range(L):
            agg = jax.ops.segment_sum(x[src], dst, num_segments=n)
            h = x + agg
            h = _prelu(h @ conv_W1[l].T + conv_b1[l], conv_a[l])
            h = h @ conv_W2[l].T + conv_b2[l]
            mean = h.mean(axis=0)
            var = ((h - mean) ** 2).mean(axis=0)
            h = (h - mean) * jax.lax.rsqrt(var + BN_EPS) * bn_gamma[l] + bn_beta[l]
            x = jax.nn.relu(h)
        return x

    def _L2_gnn_ref(X, W, b, edge_index):
        import jax, jax.numpy as jnp
        import numpy as np
        N_NODES = 6250
        EMBED_DIM = 512
        N_EDGES = 100000
        NEG_SLOPE = 0.01
        N = X.shape[0]
        loop = jnp.arange(N, dtype=edge_index.dtype)
        src = jnp.concatenate([edge_index[0], loop])
        dst = jnp.concatenate([edge_index[1], loop])
        deg = jax.ops.segment_sum(jnp.ones_like(dst, dtype=X.dtype), dst, num_segments=N)
        dinv = jnp.where(deg > 0, jax.lax.rsqrt(deg), 0.0)
        norm = dinv[src] * dinv[dst]
        H = X @ W
        msgs = H[src] * norm[:, None]
        out = jax.ops.segment_sum(msgs, dst, num_segments=N) + b
        return jnp.where(out >= 0, out, NEG_SLOPE * out)

    def _L3_gnn_ref(x, edge_index, edge_type, basis1, att1, gate_w1, root1, bias1, basis2, att2, gate_w2, root2, bias2):
        import jax, jax.numpy as jnp
        import numpy as np
        NUM_RELATIONS = 2
        NUM_BASES = 30
        HIDDEN = 512
        N_NODES = 1250
        N_EDGES = 20000

        def rgcn_gate_layer(x, row, col, edge_type, basis, att, gate_w, root, bias):
            H = x.shape[1]
            w = jnp.einsum('rb,bio->rio', att, basis)
            x_j = x[col]
            msgs = []
            for r in range(NUM_RELATIONS):
                gate = jax.nn.sigmoid(x_j @ gate_w[r, :, 0])
                msgs.append(gate[:, None] * x_j @ w[r])
            msg = jnp.where((edge_type == 0)[:, None], msgs[0], msgs[1])
            agg = jax.ops.segment_sum(msg, row, num_segments=x.shape[0])
            return agg + x @ root + bias
        row, col = (edge_index[0], edge_index[1])
        h = jax.nn.relu(rgcn_gate_layer(x, row, col, edge_type, basis1, att1, gate_w1, root1, bias1))
        out = rgcn_gate_layer(h, row, col, edge_type, basis2, att2, gate_w2, root2, bias2)
        return out
    edge_index = jnp.stack([src, dst])
    h = jnp.maximum(_layernorm(x, axis=-1), 0.0)
    x = x + _L0_gnn_ref(h, edge_index, L0_gnn_Wq, L0_gnn_bq, L0_gnn_Wk, L0_gnn_bk, L0_gnn_Wv, L0_gnn_bv, L0_gnn_Wo, L0_gnn_bo, L0_gnn_W1, L0_gnn_b1, L0_gnn_W2, L0_gnn_b2, L0_gnn_g1, L0_gnn_be1, L0_gnn_g2, L0_gnn_be2)
    h = jnp.maximum(_layernorm(x, axis=-1), 0.0)
    x = x + _L1_gnn_ref(h, edge_index, L1_gnn_lin_W, L1_gnn_lin_b, L1_gnn_lin_a, L1_gnn_conv_W1, L1_gnn_conv_b1, L1_gnn_conv_a, L1_gnn_conv_W2, L1_gnn_conv_b2, L1_gnn_bn_gamma, L1_gnn_bn_beta)
    h = jnp.maximum(_layernorm(x, axis=-1), 0.0)
    x = x + _L2_gnn_ref(h, L2_gnn_W, L2_gnn_b, edge_index)
    h = jnp.maximum(_layernorm(x, axis=-1), 0.0)
    x = x + _L3_gnn_ref(h, edge_index, edge_type_2, L3_gnn_basis1, L3_gnn_att1, L3_gnn_gate_w1, L3_gnn_root1, L3_gnn_bias1, L3_gnn_basis2, L3_gnn_att2, L3_gnn_gate_w2, L3_gnn_root2, L3_gnn_bias2)
    return x

_drawn_inputs = setup_inputs


def setup_inputs(seed=0):
    import zlib

    import numpy as np

    out = dict(_drawn_inputs(seed))
    spreads = {'L0_gnn_bq': (0.0, 2.0),
     'L0_gnn_bk': (0.0, 2.0),
     'L0_gnn_bv': (0.0, 0.1),
     'L0_gnn_bo': (0.0, 2.0),
     'L0_gnn_b1': (0.0, 0.1),
     'L0_gnn_b2': (0.0, 0.1),
     'L0_gnn_g1': (1.0, 0.2),
     'L0_gnn_be1': (0.0, 0.1),
     'L0_gnn_g2': (1.0, 0.2),
     'L0_gnn_be2': (0.0, 0.1),
     'L1_gnn_lin_a': (0.25, 0.6),
     'L1_gnn_conv_a': (0.25, 0.6),
     'L1_gnn_bn_gamma': (1.0, 0.2),
     'L1_gnn_bn_beta': (0.0, 0.1),
     'L2_gnn_b': (0.0, 0.1)}
    factors = {'L0_gnn_Wq': 3.594,
     'L0_gnn_Wk': 3.971,
     'L1_gnn_conv_b1': 39.063,
     'L1_gnn_conv_b2': 64.0,
     'L3_gnn_basis1': 8.0,
     'L3_gnn_att1': 8.0,
     'L3_gnn_gate_w1': 8.0,
     'L3_gnn_root1': 8.0,
     'L3_gnn_bias1': 21.865,
     'L3_gnn_basis2': 8.0,
     'L3_gnn_att2': 8.0,
     'L3_gnn_gate_w2': 8.0,
     'L3_gnn_root2': 8.0,
     'L3_gnn_bias2': 39.253}
    for name, (base, spread) in spreads.items():
        noise = np.random.default_rng([zlib.crc32(name.encode()), seed]).standard_normal(out[name].shape)
        drawn = base * np.exp(spread * noise) if base else spread * noise
        out[name] = jnp.asarray(drawn.astype(out[name].dtype))
    for name, factor in factors.items():
        out[name] = (out[name] * factor).astype(out[name].dtype)
    return out
```

```python
from contextlib import ExitStack

import concourse.bass as bass
import numpy as np
from concourse import mybir

F32 = mybir.dt.float32
BF16 = mybir.dt.bfloat16
F16 = mybir.dt.float16
I32 = mybir.dt.int32
ALU = mybir.AluOpType
ACT = mybir.ActivationFunctionType

P = 128
N = 512
D = 512
C = D // P
HEADS = 8
HD = D // HEADS
EDGES = 16896
ECH = EDGES // P
LN_EPS = 1e-5

GROUP = 22
GROUPS = ECH // GROUP
PAIRS = GROUPS // 2
TYPE1 = 2.0 ** -12
ROUND = 1.5 * 2.0 ** 23
assert GROUPS * GROUP == ECH and GROUP * P < 1 / TYPE1 and GROUPS % 2 == 0
HOT = 4

BASES = 30
RELS = 2
KB = C * BASES
Q = RELS * C
COLT = 4
UNITS = P // COLT
BATCH = 4
BATCHES = UNITS // BATCH

WEIGHTS = ("q", "k", "v", "o", "f1a", "f1b", "f2a", "f2b", "lin",
           "c1_0", "c2_0", "c1_1", "c2_1", "gcn", "root1", "root2")
WSLOTS = 4
LAST_READ = {"q": ("q_psum", C), "k": ("k_psum", C), "v": ("v_psum", C), "o": ("o_psum", C),
             "f1a": ("ff1_psum", C), "f1b": ("ff1_psum", 2 * C), "f2a": ("ff2_psum", C),
             "f2b": ("ff2_psum", C), "lin": ("lin_psum", C), "c1_0": ("c1_0_psum", C),
             "c2_0": ("c2_0_psum", C), "c1_1": ("c1_1_psum", C)}

ROWS = ("bv", "bo", "g1", "be1", "b2", "g2", "be2", "lin_b", "lin_a", "gcn_b", "bias1", "bias2")
RSLOTS = 6

COLS = {}
for _name, _n in (("bq", C), ("bk", C), ("b1", 2 * C), ("c1b", 2 * C), ("c2b", 2 * C), ("gam", 2 * C),
                  ("bet", 2 * C), ("gw1", RELS * C), ("gw2", RELS * C)):
    COLS[_name] = sum(n for _, n in COLS.values()), _n
NCOLS = sum(n for _, n in COLS.values())


def build(nc, x, src, dst, etype, weights, rows, cols, alphas, att, basis, scratch, out):
    with ExitStack() as ctx:
        def sb(name, shape, dt=F32):
            return ctx.enter_context(nc.sbuf_tensor(name, shape, dt))

        names = {}

        def sem(name):
            if name not in names:
                names[name] = ctx.enter_context(nc.semaphore(name))
            return names[name]

        bank = [ctx.enter_context(nc.psum_tensor(f"bank{i}", [P, N], F32)) for i in range(8)]

        xr = sb("xr", [P, C, D])
        hr = sb("hr", [P, C, D])
        hT = sb("hT", [P, C, D])
        qkw = sb("qkw", [P, 2 * C, D])
        qT, kT = qkw[:, 0:C, :], qkw[:, C:2 * C, :]
        vr = sb("vr", [P, C, D])
        s01 = sb("s01", [P, 2 * C, D])
        s0, s1 = s01[:, 0:C, :], s01[:, C:2 * C, :]
        cnt = sb("cnt", [P, 2, C, N])
        adjT = sb("adjT", [P, C, N])
        wring = sb("wring", [P, WSLOTS, C, D])
        bring = sb("bring", [P, BATCH, COLT, D])
        stage = sb("stage", [P, 2, BATCH, D])
        rring = sb("rring", [P, RSLOTS, D])
        colsb = sb("colsb", [P, NCOLS])
        alph = sb("alph", [P, 2])
        attw = sb("attw", [P, 2, 32])
        ident = sb("ident", [P, P])
        bq8 = sb("bq8", [P, C])
        stat = sb("stat", [P, 8, C, 12])
        gcn_s = sb("gcn_s", [P, C, 8])
        gate = sb("gate", [P, 2, C, RELS])
        half = sb("half", [P, 3])
        softmax_tmp = sb("softmax_tmp", [P, C, N // 2])

        edge_i = vr[:, 0, 0:3 * ECH].bitcast(I32).rearrange("p (a n) -> p a n", a=3)
        edge_f = vr[:, 1, 0:3 * ECH].rearrange("p (a n) -> p a n", a=3)
        iota = vr[:, 2, 0:N // 2].bitcast(F16)
        hot_d = s0[:, 0:2, :].rearrange("p a n -> p (a n)").bitcast(BF16).rearrange("p (r n) -> p r n", r=HOT)
        hot_s = s0[:, 2:4, :].rearrange("p a n -> p (a n)").bitcast(BF16).rearrange("p (r n) -> p r n", r=HOT)
        c_a, c_b = s1, qT
        frac = kT

        def col(name, i=0, n=1):
            at = COLS[name][0]
            return colsb[:, at + i:at + i + n]

        def row(name):
            return rring[:, ROWS.index(name) % RSLOTS, :]

        def weight(name):
            return wring[:, WEIGHTS.index(name) % WSLOTS, :, :]

        def need_row(eng, name):
            i = ROWS.index(name)
            eng.wait_ge(sem(f"row_slot{i % RSLOTS}_loaded"), 16 * (i // RSLOTS + 1))

        def need_weight(eng, name):
            i = WEIGHTS.index(name)
            eng.wait_ge(sem(f"weight_slot{i % WSLOTS}_loaded"), 16 * (i // WSLOTS + 1))

        def st(use, c, a, b=None):
            return stat[:, use, c, a:(a + 1 if b is None else b)]

        def blk(t, c):
            return slice(c * t, (c + 1) * t)

        with nc.Block() as block:

            @block.sync
            def _(sp):
                for i, e in enumerate((src, dst, etype)):
                    sp.dma_start(edge_i[:, i, :], e).then_inc(sem("edges_loaded"), 16)
                sp.dma_start(xr[:, :, :], x).then_inc(sem("x_loaded"), 16)
                sp.dma_start(colsb[:, :], cols).then_inc(sem("cols_loaded"), 16)
                sp.dma_start(alph[:, :], alphas.partition_broadcast(P)).then_inc(sem("cols_loaded"), 16)

                def load_row(name):
                    i = ROWS.index(name)
                    sp.dma_start(row(name), rows[i, :].partition_broadcast(P)).then_inc(
                        sem(f"row_slot{i % RSLOTS}_loaded"), 16)

                def load_weight(name):
                    i = WEIGHTS.index(name)
                    if i >= WSLOTS:
                        last, tiles = LAST_READ[WEIGHTS[i - WSLOTS]]
                        sp.wait_ge(sem(last), tiles)
                    sp.dma_start(weight(name), weights[i]).then_inc(sem(f"weight_slot{i % WSLOTS}_loaded"), 16)

                def load_basis(b):
                    for u in range(BATCH):
                        if b:
                            sp.wait_ge(sem("basis_used"), (b - 1) * BATCH + u + 1)
                        sp.dma_start(bring[0:KB, u, :, :], basis[b * BATCH + u]).then_inc(sem(f"basis{u}_loaded"), 16)

                def store_w(b):
                    sp.wait_ge(sem("stage_ready"), (b + 1) * BATCH)
                    layer, g = divmod(b, BATCHES)
                    for j in range(COLT):
                        at = j * UNITS + g * BATCH
                        sp.dma_start(scratch[layer, at:at + BATCH, :, :].rearrange("g q o -> q g o"),
                                     stage[32 * j:32 * j + Q, b % 2, :, :]).then_inc(sem(f"w_stored{b % 2}"), 16)

                for n in ROWS[:RSLOTS]:
                    load_row(n)
                for n in WEIGHTS[:WSLOTS]:
                    load_weight(n)
                sp.wait_ge(sem("att_zero"), 1)
                for layer in range(2):
                    for c in range(C):
                        for r in range(RELS):
                            q = r * C + c
                            sp.dma_start(attw[c * BASES:(c + 1) * BASES, layer, q:q + 1],
                                         att[layer, r, :].rearrange("(b a) -> b a", a=1)).then_inc(
                                             sem("att_loaded"), 16)
                load_basis(0)
                for n in ("f1a", "f1b", "f2a"):
                    load_weight(n)
                for b in range(8):
                    load_basis(b + 1)
                    store_w(b)
                load_weight("f2b")
                sp.wait_ge(sem("v"), C)
                load_row("be2")
                sp.wait_ge(sem("h_plus_bo"), C)
                load_row("lin_b")
                load_basis(9)
                store_w(8)
                for n in ("lin", "c1_0", "c2_0", "c1_1"):
                    load_weight(n)
                sp.wait_ge(sem("h1"), C)
                load_row("lin_a")
                load_row("gcn_b")
                load_basis(10)
                store_w(9)
                load_weight("c2_1")
                sp.wait_ge(sem("h1_plus_b2"), C)
                load_row("bias1")
                load_basis(11)
                store_w(10)
                load_weight("gcn")
                load_weight("root1")
                sp.wait_ge(sem("x1"), C)
                load_row("bias2")
                load_basis(12)
                store_w(11)
                load_weight("root2")
                for b in range(12, 2 * BATCHES - 1):
                    load_basis(b + 1)
                    store_w(b)
                store_w(2 * BATCHES - 1)

                def load_w(layer):
                    for par in range(2):
                        sp.wait_ge(sem(f"w_stored{par}"), (layer + 1) * (BATCHES // 2) * COLT * 16)
                    if layer:
                        sp.wait_ge(sem("rel0_out"), C)
                    sp.dma_start(qkw[:, :, :], scratch[layer]).then_inc(sem("w_loaded"), 16)

                load_w(0)
                load_w(1)
                for c in range(C):
                    sp.wait_ge(sem("rel1_out_sum"), c + 1)
                    sp.dma_start(out[:, c, :], hr[:, c, :]).then_inc(sem("out_stored"), 16)
                sp.wait_ge(sem("out_stored"), 16 * C)

            @block.gpsimd
            def _(pool):
                pool.memset(attw[:, :, :], 0.0).then_inc(sem("att_zero"), 1)
                pool.iota(iota, [[1, N]], base=0, channel_multiplier=0,
                          allow_small_or_imprecise_dtypes=True).then_inc(sem("iota"), 1)
                pool.memset(ident[:, :], 0.0).then_inc(sem("ident0"), 1)
                pool.wait_ge(sem("ident0"), 1)
                pool.affine_select(out=ident[:, :], in_=ident[:, :], compare_op=ALU.not_equal, fill=1.0,
                                   base=0, pattern=[[-1, P]], channel_multiplier=1).then_inc(sem("ident"), 1)
                for g in range(GROUPS):
                    for c in range(C):
                        whole = (c_a, c_b)[g % 2][:, c, :]
                        pool.wait_ge(sem("whole"), g * C + c + 1)
                        if g:
                            pool.wait_ge(sem("cnt0"), (g - 1) * C + c + 1)
                            pool.tensor_tensor(cnt[:, 0, c, :], cnt[:, 0, c, :], whole, ALU.add).then_inc(
                                sem("cnt0"), 1)
                        else:
                            pool.tensor_copy(cnt[:, 0, c, :], whole).then_inc(sem("cnt0"), 1)

            @block.scalar
            def _(act):
                def root(use, c):
                    act.wait_ge(sem(f"rvar{use}"), c + 1)
                    act.activation(st(use, c, 9), st(use, c, 8), ACT.Sqrt).then_inc(sem(f"rstd{use}"), 1)

                def relu_norm(use, c, done):
                    act.wait_ge(sem(f"nbias{use}"), c + 1)
                    act.activation(hr[:, c, :], xr[:, c, :], ACT.Relu, scale=st(use, c, 9),
                                   bias=st(use, c, 10)).then_inc(sem(done), 1)

                def turn(done, dest, ready):
                    for c in range(C):
                        act.wait_ge(sem(ready), c + 1)
                        act.copy(dest[:, :, blk(P, c)],
                                 bank[4 + c % 2][:, :].rearrange("p (f n) -> p f n", f=C)).then_inc(sem(done), 1)

                def relation_scale(layer, use):
                    act.wait_ge(sem(f"gates{layer}"), 1)
                    act.activation(gate[:, layer, :, :], bank[6][:, 0:C * RELS].rearrange("p (c r) -> p c r", c=C),
                                   ACT.Sigmoid).then_inc(sem(f"sigmoid{layer}"), 1)
                    act.wait_ge(sem(f"sigmoid{layer}"), 1)
                    for c in range(C):
                        act.activation(s1[:, c, :], hr[:, c, :], ACT.Copy,
                                       scale=gate[:, layer, c, 1:2]).then_inc(sem(f"gated1_{layer}"), 1)

                def stage_w(b):
                    for u in range(BATCH):
                        n = b * BATCH + u
                        act.wait_ge(sem("basis_used"), n + 1)
                        if b >= 2 and u == 0:
                            act.wait_ge(sem(f"w_stored{b % 2}"), (b // 2) * COLT * 16)
                        act.copy(stage[:, b % 2, u, :], bank[6 + n % 2][:, :]).then_inc(sem("stage_ready"), 1)

                for c in range(C):
                    root(0, c)
                    relu_norm(0, c, "h0")
                turn("hT0", hT, "hT0_psum")
                for g in range(GROUPS):
                    for c in range(C):
                        t = (c_a, c_b)[g % 2][:, c, :]
                        act.wait_ge(sem("hot_used"), (g + 1) * GROUP)
                        if g >= 2:
                            act.wait_ge(sem("cnt0"), (g - 2) * C + c + 1)
                            act.wait_ge(sem("frac"), 2 * ((g - 2) * C + c + 1))
                        act.wait_ge(sem("half"), 1)
                        base = (g * C + c) * 2
                        act.activation(t, bank[(g % 2) * C + c][:, :], ACT.Identity,
                                       bias=half[:, 0:1]).then_inc(sem("whole_step"), 1)
                        act.wait_ge(sem("whole_step"), base + 1)
                        act.activation(t, t, ACT.Identity, bias=half[:, 1:2]).then_inc(sem("whole_step"), 1)
                        act.wait_ge(sem("whole_step"), base + 2)
                        act.activation(t, t, ACT.Identity, bias=half[:, 2:3]).then_inc(sem("whole"), 1)

                act.wait_ge(sem("cols_loaded"), 32)
                act.wait_ge(sem("bq8"), 1)
                act.wait_ge(sem("cnt0"), GROUPS * C)
                act.wait_ge(sem("frac"), 2 * GROUPS * C)
                for c in range(C):
                    act.wait_ge(sem("q_psum"), c + 1)
                    act.activation(qT[:, c, :], bank[c][:, :], ACT.Identity, scale=HD ** -0.5,
                                   bias=bq8[:, c:c + 1]).then_inc(sem("q"), 1)
                act.wait_ge(sem("cnt1"), C)
                for c in range(C):
                    act.wait_ge(sem("k_psum"), c + 1)
                    act.activation(kT[:, c, :], bank[c][:, :], ACT.Identity,
                                   bias=col("bk", c)).then_inc(sem("k"), 1)
                for it in range(2 * C):
                    act.wait_ge(sem("centred"), it + 1)
                    sc = s01[:, (it % 2) * C:(it % 2 + 1) * C, :]
                    act.activation(sc, sc, ACT.Exp).then_inc(sem("exped"), 1)
                    stage_w(it)
                act.wait_ge(sem("pv_used"), 2 * C)
                for c in range(C):
                    act.copy(s0[:, c, :], bank[c][:, :]).then_inc(sem("ao"), 1)
                for c in range(C):
                    root(1, c)
                stage_w(8)
                turn("h1T", hT, "h1T_psum")
                for t in range(2 * C):
                    act.wait_ge(sem("ff1_psum"), t + 1)
                    act.activation(s01[:, t, :], bank[t % C][:, :], ACT.Relu,
                                   bias=col("b1", t)).then_inc(sem("ff1"), 1)
                for c in range(C):
                    root(2, c)
                for c in range(C):
                    root(3, c)
                    relu_norm(3, c, "h2")
                stage_w(9)
                turn("hT2", hT, "hT2_psum")
                stage_w(10)
                for l in range(2):
                    for c in range(C):
                        act.wait_ge(sem(f"agg{l}_psum"), c + 1)
                        act.copy(hT[:, c, :], bank[c][:, :]).then_inc(sem(f"agg{l}"), 1)
                    for c in range(C):
                        act.wait_ge(sem(f"c1_{l}_psum"), c + 1)
                        act.activation(s0[:, c, :], bank[c][:, :], ACT.Identity,
                                       bias=col("c1b", l * C + c)).then_inc(sem(f"c1_{l}_sum"), 1)
                    for c in range(C):
                        act.wait_ge(sem(f"c2_{l}_psum"), c + 1)
                        act.activation(s1[:, c, :], bank[c][:, :], ACT.Identity,
                                       bias=col("c2b", l * C + c)).then_inc(sem(f"c2_{l}"), 1)
                        if c:
                            root(4 + l, c - 1)
                            act.wait_ge(sem(f"bnb{l}"), c)
                            act.activation(s1[:, c - 1, :], s1[:, c - 1, :], ACT.Relu, scale=st(4 + l, c - 1, 10),
                                           bias=st(4 + l, c - 1, 11)).then_inc(sem(f"bn{l}"), 1)
                    root(4 + l, C - 1)
                    act.wait_ge(sem(f"bnb{l}"), C)
                    act.activation(s1[:, C - 1, :], s1[:, C - 1, :], ACT.Relu, scale=st(4 + l, C - 1, 10),
                                   bias=st(4 + l, C - 1, 11)).then_inc(sem(f"bn{l}"), 1)
                    stage_w(11 + l)
                    if l == 0:
                        turn("x3", vr, "x3_psum")
                act.wait_ge(sem("deg"), 1)
                act.activation(gcn_s[:, :, 2], gcn_s[:, :, 1], ACT.Sqrt).then_inc(sem("dinv"), 1)
                for c in range(C):
                    root(6, c)
                    act.wait_ge(sem("gcn_nb"), c + 1)
                    act.activation(hr[:, c, :], xr[:, c, :], ACT.Relu, scale=gcn_s[:, c, 3:4],
                                   bias=gcn_s[:, c, 4:5]).then_inc(sem("h_gcn"), 1)
                stage_w(13)
                for c in range(C):
                    act.wait_ge(sem("agg2_psum"), c + 1)
                    act.copy(hT[:, c, :], bank[c][:, :]).then_inc(sem("agg2"), 1)
                stage_w(14)
                for c in range(C):
                    root(7, c)
                    relu_norm(7, c, "h_rel0")
                for layer in range(2):
                    turn(f"relT{layer}", hT, f"relT{layer}_psum")
                    if layer == 0:
                        stage_w(15)
                    relation_scale(layer, None)
                    for c in range(C):
                        act.wait_ge(sem(f"G{layer}_psum"), c + 1)
                        act.copy(vr[:, c, :], bank[c][:, :]).then_inc(sem(f"G0_{layer}"), 1)

            @block.vector
            def _(dve):
                steps = [0]

                def step(ins):
                    steps[0] += 1
                    ins.then_inc(sem("dve_step"), 1)
                    return steps[0]

                def after(n):
                    dve.wait_ge(sem("dve_step"), n)

                dve.memset(half[:, 0:1], -0.484375)
                dve.memset(half[:, 1:2], ROUND)
                dve.memset(half[:, 2:3], -ROUND).then_inc(sem("half"), 1)

                dve.wait_ge(sem("edges_loaded"), 48)
                dve.tensor_copy(edge_f[:, 0:2, :], edge_i[:, 0:2, :]).then_inc(sem("dve_step"), 1)
                dve.tensor_scalar(edge_f[:, 2, :], edge_i[:, 2, :], 0.0, 1.0 - TYPE1, ALU.is_equal,
                                  ALU.mult).then_inc(sem("dve_step"), 1)
                after(2)
                dve.tensor_scalar(edge_f[:, 2, :], edge_f[:, 2, :], TYPE1, None, ALU.add).then_inc(
                    sem("dve_step"), 1)
                after(3)
                steps[0] = 3
                dve.wait_ge(sem("iota"), 1)

                def one_hots(n, k, first):
                    if not first:
                        dve.wait_ge(sem("hot_used"), n - HOT + 1)
                    dve.tensor_scalar(hot_d[:, k % HOT, :], iota, edge_f[:, 1, bass.ds(n, 1)], None,
                                      ALU.is_equal).then_inc(sem("hot_ready"), 1)
                    dve.tensor_scalar(hot_s[:, k % HOT, :], iota, edge_f[:, 0, bass.ds(n, 1)],
                                      edge_f[:, 2, bass.ds(n, 1)], ALU.is_equal, ALU.mult).then_inc(
                                          sem("hot_ready"), 1)

                def fractions(g):
                    for c in range(C):
                        whole = (c_a, c_b)[g % 2][:, c, :]
                        v = bank[(g % 2) * C + c][:, :]
                        f = frac[:, c, :]
                        n = g * C + c
                        dve.wait_ge(sem("whole"), n + 1)
                        if g:
                            dve.wait_ge(sem("frac"), 2 * ((g - 1) * C + c + 1))
                            dve.tensor_tensor(f, f, whole, ALU.add).then_inc(sem("frac"), 1)
                        else:
                            dve.tensor_copy(f, whole).then_inc(sem("frac"), 1)
                        dve.wait_ge(sem("frac"), 2 * n + 1)
                        dve.tensor_tensor(f, f, v, ALU.subtract).then_inc(sem("frac"), 1)

                def norm_stats(use, t, c, width=1):
                    dve.bn_stats(st(use, c, 0, 6), t).then_inc(sem("dve_step"), 1)
                    steps[0] += 1
                    after(steps[0])
                    after(step(dve.bn_aggr(st(use, c, 6, 8), st(use, c, 0, 6))))
                    after(step(dve.tensor_scalar(st(use, c, 7), st(use, c, 7), LN_EPS, None, ALU.add)))
                    dve.reciprocal(st(use, c, 8), st(use, c, 7)).then_inc(sem(f"rvar{use}"), 1)

                def nbias(use, c):
                    dve.wait_ge(sem(f"rstd{use}"), c + 1)
                    dve.tensor_scalar(st(use, c, 10), st(use, c, 6), st(use, c, 9), -1.0, ALU.mult,
                                      ALU.mult).then_inc(sem(f"nbias{use}"), 1)

                def relu_norm_stats(use, ready):
                    for c in range(C):
                        if ready:
                            dve.wait_ge(sem(ready), c + 1)
                        norm_stats(use, xr[:, c, :], c)
                        nbias(use, c)

                for k in range(HOT):
                    one_hots(k, k, True)
                for g in range(GROUPS):
                    lo = HOT if g == 0 else g * GROUP
                    for n in range(lo, (g + 1) * GROUP):
                        one_hots(n, n, False)
                        if n == GROUP // 2:
                            dve.wait_ge(sem("x_loaded"), 16)
                            relu_norm_stats(0, None)
                        if g and n == g * GROUP + GROUP // 2:
                            fractions(g - 1)

                fractions(GROUPS - 1)
                dve.wait_ge(sem("cols_loaded"), 32)
                dve.tensor_scalar(bq8[:, :], col("bq", 0, C), HD ** -0.5, None, ALU.mult).then_inc(sem("bq8"), 1)
                for c in range(C):
                    dve.wait_ge(sem("frac"), 2 * ((GROUPS - 1) * C + c + 1))
                    dve.tensor_scalar(cnt[:, 1, c, :], frac[:, c, :], -1.0 / TYPE1, None, ALU.mult).then_inc(
                        sem("cnt1"), 1)
                for c in range(C):
                    dve.wait_ge(sem("cnt1"), c + 1)
                    dve.wait_ge(sem("cnt0"), (GROUPS - 1) * C + c + 1)
                    after(step(dve.tensor_tensor(adjT[:, c, :], cnt[:, 0, c, :], cnt[:, 1, c, :], ALU.add)))
                    dve.tensor_scalar(adjT[:, c, :], adjT[:, c, :], 0.0, None, ALU.is_gt).then_inc(sem("mask"), 1)
                need_row(dve, "bv")
                for c in range(C):
                    dve.wait_ge(sem("v_psum"), c + 1)
                    dve.tensor_tensor(vr[:, c, :], bank[c][:, :], row("bv"), ALU.add).then_inc(sem("v"), 1)
                need_row(dve, "bo")
                for c in range(C):
                    dve.wait_ge(sem("hT0_psum"), c + 1)
                    dve.tensor_tensor(hr[:, c, :], hr[:, c, :], row("bo"), ALU.add).then_inc(sem("h_plus_bo"), 1)
                NH = N // 2
                tmp = softmax_tmp
                for it in range(2 * C):
                    half_n, m = divmod(it, C)
                    sc = s01[:, (it % 2) * C:(it % 2 + 1) * C, :].rearrange("p c (a n) -> p (c a) n", a=2)
                    if it >= 2:
                        dve.wait_ge(sem("pv_used"), it - 1)
                    if it == 0:
                        dve.wait_ge(sem("mask"), C)
                    mask = adjT[:, m, blk(NH, half_n)].unsqueeze(1).to_broadcast([P, 2, NH])
                    for q in range(4):
                        h0 = 4 * (q // 2) + q % 2
                        dve.wait_ge(sem("scores_psum"), it * 4 + q + 1)
                        ins = dve.tensor_tensor(sc[:, h0:h0 + 3:2, :],
                                                bank[4 + q % 2][:, :].rearrange("p (a n) -> p a n", a=2),
                                                mask, ALU.mult)
                        ins.then_inc(sem("scores"), 1)
                    dve.wait_ge(sem("scores"), 4 * it + 4)
                    after(step(dve.tensor_tensor(tmp[:, 0:4, :], sc[:, 0:4, :], sc[:, 4:8, :], ALU.max)))
                    after(step(dve.tensor_tensor(tmp[:, 0:2, :], tmp[:, 0:2, :], tmp[:, 2:4, :], ALU.max)))
                    after(step(dve.tensor_tensor(tmp[:, 0, :], tmp[:, 0, :], tmp[:, 1, :], ALU.max)))
                    dve.tensor_tensor(sc, sc, tmp[:, 0:1, :].to_broadcast([P, HEADS, NH]),
                                      ALU.subtract).then_inc(sem("centred"), 1)
                    dve.wait_ge(sem("exped"), it + 1)
                    after(step(dve.tensor_tensor(tmp[:, 0:4, :], sc[:, 0:4, :], sc[:, 4:8, :], ALU.add)))
                    after(step(dve.tensor_tensor(tmp[:, 0:2, :], tmp[:, 0:2, :], tmp[:, 2:4, :], ALU.add)))
                    after(step(dve.tensor_tensor(tmp[:, 0, :], tmp[:, 0, :], tmp[:, 1, :], ALU.add)))
                    after(step(dve.reciprocal(tmp[:, 1, :], tmp[:, 0, :])))
                    dve.tensor_tensor(sc, sc, tmp[:, 1:2, :].to_broadcast([P, HEADS, NH]),
                                      ALU.mult).then_inc(sem("probs"), 1)
                dve.wait_ge(sem("pv_used"), 2 * C)
                dve.wait_ge(sem("ident"), 1)
                for c in range(C):
                    after(step(dve.tensor_tensor(s1[:, c, :], cnt[:, 0, c, :], cnt[:, 1, c, :], ALU.add)))
                    dve.tensor_tensor(s1[:, c, blk(P, c)], s1[:, c, blk(P, c)], ident[:, :],
                                      ALU.add).then_inc(sem("adj"), 1)
                for c in range(C):
                    dve.wait_ge(sem("adj"), c + 1)
                    n = step(dve.reduce_sum(gcn_s[:, c, 0:1], s1[:, c, :], axis=mybir.AxisListType.X))
                after(n)
                dve.reciprocal(gcn_s[:, :, 1], gcn_s[:, :, 0]).then_inc(sem("deg"), 1)
                for c in range(C):
                    dve.wait_ge(sem("adjT_psum"), c + 1)
                    dve.tensor_copy(adjT[:, :, blk(P, c)],
                                    bank[4 + c % 2][:, :].rearrange("p (f n) -> p f n", f=C)).then_inc(
                                        sem("adjT"), 1)

                def affine_norm(use, t, c, g, be, dest, done):
                    dve.wait_ge(sem(f"rvar{use}"), c + 1)
                    after(step(dve.scalar_tensor_tensor(t, t, st(use, c, 6), row(g), ALU.subtract, ALU.mult)))
                    dve.wait_ge(sem(f"rstd{use}"), c + 1)
                    dve.scalar_tensor_tensor(dest, t, st(use, c, 9), be, ALU.mult, ALU.add).then_inc(sem(done), 1)

                for n in ("g1", "be1", "b2", "g2"):
                    need_row(dve, n)
                for c in range(C):
                    dve.wait_ge(sem("o_psum"), c + 1)
                    after(step(dve.tensor_tensor(vr[:, c, :], bank[c][:, :], hr[:, c, :], ALU.add)))
                    norm_stats(1, vr[:, c, :], c)
                    affine_norm(1, vr[:, c, :], c, "g1", row("be1"), vr[:, c, :], "h1")
                for c in range(C):
                    dve.wait_ge(sem("h1T_psum"), c + 1)
                    dve.tensor_tensor(vr[:, c, :], vr[:, c, :], row("b2"), ALU.add).then_inc(sem("h1_plus_b2"), 1)
                need_row(dve, "be2")
                for c in range(C):
                    dve.wait_ge(sem("h0"), c + 1)
                    dve.tensor_tensor(xr[:, c, :], xr[:, c, :], row("be2"), ALU.add).then_inc(sem("x_plus"), 1)
                for c in range(C):
                    dve.wait_ge(sem("ff2_psum"), c + 1)
                    dve.wait_ge(sem("h1_plus_b2"), c + 1)
                    after(step(dve.tensor_tensor(hr[:, c, :], bank[c][:, :], vr[:, c, :], ALU.add)))
                    norm_stats(2, hr[:, c, :], c)
                    dve.wait_ge(sem("x_plus"), c + 1)
                    affine_norm(2, hr[:, c, :], c, "g2", xr[:, c, :], xr[:, c, :], "x1")
                relu_norm_stats(3, "x1")
                need_row(dve, "lin_b")
                need_row(dve, "lin_a")
                for c in range(C):
                    dve.wait_ge(sem("lin_psum"), c + 1)
                    after(step(dve.tensor_tensor(s1[:, c, :], bank[c][:, :], row("lin_b"), ALU.add)))
                    after(step(dve.scalar_tensor_tensor(s0[:, c, :], s1[:, c, :], 0.0, row("lin_a"),
                                                        ALU.min, ALU.mult)))
                    dve.scalar_tensor_tensor(vr[:, c, :], s1[:, c, :], 0.0, s0[:, c, :], ALU.max,
                                             ALU.add).then_inc(sem("x2"), 1)
                for l in range(2):
                    for c in range(C):
                        dve.wait_ge(sem(f"c1_{l}_sum"), c + 1)
                        after(step(dve.tensor_scalar(vr[:, c, :], s0[:, c, :], 0.0, alph[:, l:l + 1], ALU.min,
                                                     ALU.mult)))
                        dve.scalar_tensor_tensor(s0[:, c, :], s0[:, c, :], 0.0, vr[:, c, :], ALU.max,
                                                 ALU.add).then_inc(sem(f"c1_{l}"), 1)
                    for c in range(C):
                        dve.wait_ge(sem(f"c2_{l}"), c + 1)
                        norm_stats(4 + l, s1[:, c, :], c)
                        dve.wait_ge(sem(f"rstd{4 + l}"), c + 1)
                        after(step(dve.tensor_scalar(st(4 + l, c, 10), st(4 + l, c, 9), col("gam", l * C + c), None,
                                                     ALU.mult)))
                        after(step(dve.tensor_scalar(st(4 + l, c, 11), st(4 + l, c, 6), st(4 + l, c, 10), -1.0,
                                                     ALU.mult, ALU.mult)))
                        dve.tensor_scalar(st(4 + l, c, 11), st(4 + l, c, 11), col("bet", l * C + c), None,
                                          ALU.add).then_inc(sem(f"bnb{l}"), 1)
                for c in range(C):
                    dve.wait_ge(sem("x4_psum"), c + 1)
                    dve.tensor_tensor(xr[:, c, :], xr[:, c, :], bank[4 + c % 2][:, :], ALU.add).then_inc(
                        sem("x5"), 1)
                for c in range(C):
                    dve.wait_ge(sem("x5"), c + 1)
                    norm_stats(6, xr[:, c, :], c)
                    dve.wait_ge(sem("dinv"), 1)
                    dve.wait_ge(sem("rstd6"), c + 1)
                    after(step(dve.tensor_scalar(gcn_s[:, c, 3:4], st(6, c, 9), gcn_s[:, c, 2:3], None, ALU.mult)))
                    dve.tensor_scalar(gcn_s[:, c, 4:5], st(6, c, 6), gcn_s[:, c, 3:4], -1.0, ALU.mult,
                                      ALU.mult).then_inc(sem("gcn_nb"), 1)
                need_row(dve, "gcn_b")
                for c in range(C):
                    dve.wait_ge(sem("gcn_psum"), c + 1)
                    after(step(dve.scalar_tensor_tensor(s0[:, c, :], bank[c][:, :], gcn_s[:, c, 2:3], row("gcn_b"),
                                                        ALU.mult, ALU.add)))
                    after(step(dve.scalar_tensor_tensor(s1[:, c, :], s0[:, c, :], 0.01, s0[:, c, :], ALU.mult,
                                                        ALU.max)))
                    dve.wait_ge(sem("h_gcn"), c + 1)
                    dve.tensor_tensor(xr[:, c, :], xr[:, c, :], s1[:, c, :], ALU.add).then_inc(sem("x6"), 1)
                    dve.wait_ge(sem("x6"), c + 1)
                    norm_stats(7, xr[:, c, :], c)
                    nbias(7, c)
                need_row(dve, "bias1")
                need_row(dve, "bias2")
                for layer in range(2):
                    dve.wait_ge(sem(f"sigmoid{layer}"), 1)
                    for c in range(C):
                        dve.tensor_scalar(s0[:, c, :], hr[:, c, :], gate[:, layer, c, 0:1], None,
                                          ALU.mult).then_inc(sem(f"gated0_{layer}"), 1)
                    if layer == 0:
                        for c in range(C):
                            dve.wait_ge(sem("h_rel0"), c + 1)
                            dve.tensor_tensor(xr[:, c, :], xr[:, c, :], row("bias2"), ALU.add).then_inc(
                                sem("x_plus_bias2"), 1)
                    for c in range(C):
                        dve.wait_ge(sem(f"G{layer}_psum"), C + c + 1)
                        dve.tensor_copy(adjT[:, c, :], bank[c][:, :]).then_inc(sem(f"G1_{layer}"), 1)
                    for c in range(C):
                        dve.wait_ge(sem(f"rel{layer}_psum"), c + 1)
                        if layer == 0:
                            dve.wait_ge(sem("gated1_0"), C)
                            dve.wait_ge(sem("gated0_0"), C)
                            after(step(dve.tensor_tensor(hr[:, c, :], bank[c][:, :], row("bias1"), ALU.add)))
                            dve.tensor_scalar(hr[:, c, :], hr[:, c, :], 0.0, None, ALU.max).then_inc(
                                sem("rel0_out"), 1)
                        else:
                            dve.wait_ge(sem("gated1_1"), C)
                            dve.wait_ge(sem("gated0_1"), C)
                            dve.wait_ge(sem("x_plus_bias2"), c + 1)
                            dve.tensor_tensor(hr[:, c, :], bank[c][:, :], xr[:, c, :], ALU.add).then_inc(
                                sem("rel1_out_sum"), 1)

            @block.tensor
            def _(pe):
                def turn(src, ready, done, free, free_n=None):
                    for c in range(C):
                        if ready:
                            pe.wait_ge(sem(ready), c + 1)
                        if c < 2:
                            if free:
                                pe.wait_ge(sem(free), free_n or C)
                        else:
                            pe.wait_ge(sem(done.removesuffix("_psum")), c - 1)
                        for f in range(C):
                            mm = pe.transpose(bank[4 + c % 2][:, blk(P, f)], src[:, c, blk(P, f)], ident[:, :])
                        mm.then_inc(sem(done), 1)

                def batch(b):
                    layer = b // BATCHES
                    if b == 0:
                        pe.wait_ge(sem("att_loaded"), 16 * 2 * Q)
                    for u in range(BATCH):
                        n = b * BATCH + u
                        if n >= 2:
                            pe.wait_ge(sem("stage_ready"), n - 1)
                        pe.wait_ge(sem(f"basis{u}_loaded"), 16 * (b + 1))
                        for j in range(COLT):
                            mm = pe.matmul(bank[6 + n % 2][32 * j:32 * j + 32, :], attw[0:KB, layer, :],
                                           bring[0:KB, u, j, :], start=True, stop=True,
                                           tile_position=(0, 32 * j))
                        mm.then_inc(sem("basis_used"), 1)

                for g in range(GROUPS):
                    if g >= 2:
                        pe.wait_ge(sem("frac"), 2 * (g - 1) * C)
                    for k in range(GROUP):
                        n = g * GROUP + k
                        pe.wait_ge(sem("hot_ready"), 2 * n + 2)
                        for c in range(C):
                            mm = pe.matmul(bank[(g % 2) * C + c][:, :], hot_d[:, n % HOT, blk(P, c)],
                                           hot_s[:, n % HOT, :], start=(k == 0), stop=(k == GROUP - 1))
                        mm.then_inc(sem("hot_used"), 1)
                    if g == 0:
                        pe.wait_ge(sem("ident"), 1)
                        turn(hr, "h0", "hT0_psum", None)
                        pe.wait_ge(sem("hT0"), C)

                def stage_T(wname, rhs, rhs_ready, done, tiles=range(C), first_free=None):
                    need_weight(pe, wname)
                    w = weight(wname)
                    for c in tiles:
                        if first_free:
                            pe.wait_ge(sem(first_free), c % C + 1)
                        mm = None
                        for k in range(C):
                            if rhs_ready and c == tiles[0]:
                                pe.wait_ge(sem(rhs_ready), k + 1)
                            mm = pe.matmul(bank[c % C][:, :], w[:, k, blk(P, c % C)], rhs[:, k, :],
                                           start=(k == 0), stop=(k == C - 1))
                        mm.then_inc(sem(done), 1)

                def stage_row(wname, lhs, lhs_ready, done, first_free=None):
                    need_weight(pe, wname)
                    w = weight(wname)
                    for c in range(C):
                        if first_free:
                            pe.wait_ge(sem(first_free), c + 1)
                        for k in range(C):
                            if c == 0 and lhs_ready:
                                pe.wait_ge(sem(lhs_ready), k + 1)
                            mm = pe.matmul(bank[c][:, :], lhs[:, k, blk(P, c)], w[:, k, :],
                                           start=(k == 0), stop=(k == C - 1))
                        mm.then_inc(sem(done), 1)

                def aggregate(lhs, ready, done, free=None):
                    for f in range(C):
                        if free:
                            pe.wait_ge(sem(free), f + 1)
                        for k in range(C):
                            if f == 0:
                                pe.wait_ge(sem(ready), k + 1)
                            mm = pe.matmul(bank[f][:, :], lhs[:, k, blk(P, f)], adjT[:, k, :],
                                           start=(k == 0), stop=(k == C - 1))
                        mm.then_inc(sem(done), 1)

                pe.wait_ge(sem("cols_loaded"), 32)
                pe.wait_ge(sem("frac"), 2 * (GROUPS - 1) * C)
                stage_T("q", hT, None, "q_psum")
                stage_T("k", hT, None, "k_psum", first_free="q")
                stage_row("v", hT, None, "v_psum", first_free="k")
                pe.wait_ge(sem("v"), C)
                pe.wait_ge(sem("frac"), 2 * GROUPS * C)
                NH = N // 2
                for it in range(2 * C + 1):
                    if it < 2 * C:
                        half_n, m = divmod(it, C)
                        if it == 0:
                            pe.wait_ge(sem("k"), C)
                        for q in range(4):
                            h0 = 4 * (q // 2) + q % 2
                            at = 64 * (q % 2)
                            if it or q >= 2:
                                pe.wait_ge(sem("scores"), it * 4 + q - 1)
                            for a in range(2):
                                t = (h0 + 2 * a) // 2
                                mm = pe.matmul(bank[4 + q % 2][:, blk(NH, a)], kT[at:at + HD, t, blk(P, m)],
                                               qT[at:at + HD, t, blk(NH, half_n)], start=True, stop=True)
                            mm.then_inc(sem("scores_psum"), 1)
                    if it:
                        half_p, mp = divmod(it - 1, C)
                        sc = s01[:, ((it - 1) % 2) * C:((it - 1) % 2 + 1) * C, :].rearrange(
                            "p c (a n) -> p (c a) n", a=2)
                        batch(it - 1)
                        pe.wait_ge(sem("probs"), it)
                        for h in range(HEADS):
                            at = 64 * (h % 2)
                            mm = pe.matmul(bank[h // 2][at:at + HD, blk(NH, half_p)],
                                           vr[:, mp, blk(HD, h)], sc[:, h, :],
                                           start=(mp == 0), stop=(mp == C - 1), skip_group_check=True)
                        mm.then_inc(sem("pv_used"), 1)
                stage_row("o", s0, "ao", "o_psum")
                turn(s1, "adj", "adjT_psum", "scores", 8 * C)
                batch(8)
                turn(vr, "h1", "h1T_psum", "adjT", C)
                pe.wait_ge(sem("h1T"), C)
                stage_T("f1a", hT, None, "ff1_psum")
                stage_T("f1b", hT, None, "ff1_psum", tiles=range(C, 2 * C), first_free="ff1")
                need_weight(pe, "f2a")
                need_weight(pe, "f2b")
                for c in range(C):
                    pe.wait_ge(sem("ff1"), C + c + 1)
                    if c == 0:
                        pe.wait_ge(sem("ff1"), 2 * C)
                    for k in range(2 * C):
                        w = weight("f2a" if k < C else "f2b")
                        mm = pe.matmul(bank[c][:, :], s01[:, k, blk(P, c)], w[:, k % C, :],
                                       start=(k == 0), stop=(k == 2 * C - 1))
                    mm.then_inc(sem("ff2_psum"), 1)
                batch(9)
                turn(hr, "h2", "hT2_psum", "h1T", C)
                pe.wait_ge(sem("hT2"), C)
                stage_row("lin", hT, None, "lin_psum", first_free="x1")
                batch(10)
                pe.wait_ge(sem("adjT"), C)
                aggregate(vr, "x2", "agg0_psum")
                for l in range(2):
                    if l:
                        aggregate(vr, "x3", "agg1_psum")
                    stage_T(f"c1_{l}", hT, f"agg{l}", f"c1_{l}_psum")
                    stage_T(f"c2_{l}", s0, f"c1_{l}", f"c2_{l}_psum")
                    batch(11 + l)
                    if l == 0:
                        turn(s1, "bn0", "x3_psum", "hT2", C)
                    else:
                        for c in range(C):
                            if c == 0:
                                pe.wait_ge(sem("bn1"), C)
                                pe.wait_ge(sem("x3"), C)
                            if c >= 2:
                                pe.wait_ge(sem("x5"), c - 1)
                            for f in range(C):
                                mm = pe.transpose(bank[4 + c % 2][:, blk(P, f)], s1[:, f, blk(P, c)], ident[:, :])
                            mm.then_inc(sem("x4_psum"), 1)
                batch(13)
                aggregate(hr, "h_gcn", "agg2_psum", free=None)
                stage_row("gcn", hT, "agg2", "gcn_psum")
                batch(14)
                for layer in range(2):
                    if layer == 0:
                        turn(hr, "h_rel0", "relT0_psum", "x5", C)
                        batch(15)
                    else:
                        turn(hr, "rel0_out", "relT1_psum", "relT0", C)
                    pe.wait_ge(sem(f"relT{layer}"), C)
                    pe.wait_ge(sem("stage_ready"), 2 * UNITS)
                    for c in range(C):
                        for k in range(C):
                            mm = pe.matmul(bank[6][:, c * RELS:(c + 1) * RELS], hT[:, k, blk(P, c)],
                                           col(f"gw{layer + 1}", k * RELS, RELS),
                                           start=(k == 0), stop=(k == C - 1))
                    mm.then_inc(sem(f"gates{layer}"), 1)
                    for r, g in ((0, s0), (1, s1)):
                        for f in range(C):
                            if r:
                                pe.wait_ge(sem(f"G0_{layer}"), f + 1)
                            for k in range(C):
                                if f == 0:
                                    pe.wait_ge(sem(f"gated{r}_{layer}"), k + 1)
                                mm = pe.matmul(bank[f][:, :], g[:, k, blk(P, f)], cnt[:, r, k, :],
                                               start=(k == 0), stop=(k == C - 1))
                            mm.then_inc(sem(f"G{layer}_psum"), 1)
                    wname = f"root{layer + 1}"
                    need_weight(pe, wname)
                    w = weight(wname)
                    for c in range(C):
                        pe.wait_ge(sem(f"G1_{layer}"), c + 1)
                        for k in range(C):
                            pe.matmul(bank[c][:, :], hT[:, k, blk(P, c)], w[:, k, :], start=(k == 0), stop=False)
                        if c == 0:
                            pe.wait_ge(sem("w_loaded"), 16 * (layer + 1))
                            pe.wait_ge(sem(f"G1_{layer}"), C)
                        for r, g in ((0, vr), (1, adjT)):
                            for k in range(C):
                                mm = pe.matmul(bank[c][:, :], g[:, k, blk(P, c)], qkw[:, r * C + k, :],
                                               start=False, stop=(r == 1 and k == C - 1))
                        mm.then_inc(sem(f"rel{layer}_psum"), 1)


def _chunked(w):
    return np.ascontiguousarray(w.reshape(C, P, -1).transpose(1, 0, 2))


def kernel(**inputs):
    import concourse.bacc as bacc
    from concourse.bass_utils import run_bass_kernel_spmd

    i = {k: np.asarray(v) for k, v in inputs.items()}
    edge = {k: np.ascontiguousarray(i[k].reshape(ECH, P).T) for k in ("src", "dst", "edge_type_2")}
    w1, w2 = i["L0_gnn_W1"], i["L0_gnn_W2"]
    conv1, conv2 = i["L1_gnn_conv_W1"], i["L1_gnn_conv_W2"]
    weights = np.stack([_chunked(w) for w in (
        i["L0_gnn_Wq"], i["L0_gnn_Wk"], i["L0_gnn_Wv"], i["L0_gnn_Wo"], w1[:, :D], w1[:, D:], w2[:D], w2[D:],
        i["L1_gnn_lin_W"].T, conv1[0].T, conv2[0].T, conv1[1].T, conv2[1].T,
        i["L2_gnn_W"], i["L3_gnn_root1"], i["L3_gnn_root2"])])
    rows = np.stack([i[k] for k in (
        "L0_gnn_bv", "L0_gnn_bo", "L0_gnn_g1", "L0_gnn_be1", "L0_gnn_b2", "L0_gnn_g2", "L0_gnn_be2",
        "L1_gnn_lin_b", "L1_gnn_lin_a", "L2_gnn_b", "L3_gnn_bias1", "L3_gnn_bias2")])
    cols = np.concatenate([i[k].reshape(-1, P).T for k in (
        "L0_gnn_bq", "L0_gnn_bk", "L0_gnn_b1", "L1_gnn_conv_b1", "L1_gnn_conv_b2", "L1_gnn_bn_gamma",
        "L1_gnn_bn_beta")] + [
            i[k][:, :, 0].reshape(RELS, C, P).transpose(2, 1, 0).reshape(P, -1)
            for k in ("L3_gnn_gate_w1", "L3_gnn_gate_w2")], axis=1)
    basis = np.concatenate([
        i[k].reshape(BASES, C, COLT, UNITS, D).transpose(3, 1, 0, 2, 4).reshape(UNITS, KB, COLT, D)
        for k in ("L3_gnn_basis1", "L3_gnn_basis2")])
    att = np.stack([i["L3_gnn_att1"], i["L3_gnn_att2"]])
    arrays = {"x": _chunked(i["x"]), "src": edge["src"], "dst": edge["dst"], "etype": edge["edge_type_2"],
              "weights": weights, "rows": rows, "cols": cols, "alphas": i["L1_gnn_conv_a"], "att": att,
              "basis": basis}
    arrays = {k: np.ascontiguousarray(a) for k, a in arrays.items()}

    nc = bacc.Bacc("TRN2", target_bir_lowering=False, num_devices=1)
    args = [nc.dram_tensor(f"in_{k}", a.shape, mybir.dt.from_np(a.dtype), kind="ExternalInput").ap()
            for k, a in arrays.items()]
    scratch = nc.dram_tensor("w_scratch", (2, P, Q, D), F32, kind="Internal").ap()
    out = nc.dram_tensor("out_0", (P, C, D), F32, kind="ExternalOutput").ap()
    build(nc, *args, scratch, out)
    r = run_bass_kernel_spmd(nc, [{f"in_{k}": a for k, a in arrays.items()}], core_ids=[0])
    return np.ascontiguousarray(r.results[0]["out_0"].transpose(1, 0, 2)).reshape(N, D)
```

```python
from contextlib import ExitStack

import concourse.bass as bass
import numpy as np
from concourse import mybir

F32 = mybir.dt.float32
BF16 = mybir.dt.bfloat16
F16 = mybir.dt.float16
I32 = mybir.dt.int32
ALU = mybir.AluOpType
ACT = mybir.ActivationFunctionType

P = 128
N = 512
D = 512
C = D // P
HEADS = 8
HD = D // HEADS
EDGES = 16896
ECH = EDGES // P
LN_EPS = 1e-5

FIELDS = 2 * C
FBITS = 3
UNIT_BITS = FBITS * (FIELDS - 1)
TOO_MANY = 1.0e6
HOT = 16
FIRST_TILE, TILE_EVERY = 48, 9
assert EDGES % P == 0 and FBITS * FIELDS <= 24

BASES = 30
RELS = 2
KB = C * BASES
Q = RELS * C
COLT = 4
UNITS = P // COLT
BATCH = 4
BATCHES = UNITS // BATCH

WEIGHTS = ("q", "k", "v", "o", "f1a", "f1b", "f2a", "f2b", "lin",
           "c1_0", "c2_0", "c1_1", "c2_1", "gcn", "root1", "root2")
WSLOTS = 4
LAST_READ = {"q": ("q_psum", C), "k": ("k_psum", C), "v": ("v_psum", C), "o": ("o_psum", C),
             "f1a": ("ff1_psum", C), "f1b": ("ff1_psum", 2 * C), "f2a": ("ff2_psum", C),
             "f2b": ("ff2_psum", C), "lin": ("lin_psum", C), "c1_0": ("c1_0_psum", C),
             "c2_0": ("c2_0_psum", C), "c1_1": ("c1_1_psum", C)}

ROWS = ("bv", "bo", "g1", "be1", "b2", "g2", "be2", "lin_b", "lin_a", "gcn_b", "bias1", "bias2")
RSLOTS = 6

COLS = {}
for _name, _n in (("bq", C), ("bk", C), ("b1", 2 * C), ("c1b", 2 * C), ("c2b", 2 * C), ("gam", 2 * C),
                  ("bet", 2 * C), ("gw1", RELS * C), ("gw2", RELS * C)):
    COLS[_name] = sum(n for _, n in COLS.values()), _n
NCOLS = sum(n for _, n in COLS.values())


def build(nc, x, src, dst, etype, weights, rows, cols, alphas, att, basis, scratch, out):
    with ExitStack() as ctx:
        def sb(name, shape, dt=F32):
            return ctx.enter_context(nc.sbuf_tensor(name, shape, dt))

        names = {}

        def sem(name):
            if name not in names:
                names[name] = ctx.enter_context(nc.semaphore(name))
            return names[name]

        bank = [ctx.enter_context(nc.psum_tensor(f"bank{i}", [P, N], F32)) for i in range(8)]

        xr = sb("xr", [P, C, D])
        hr = sb("hr", [P, C, D])
        hT = sb("hT", [P, C, D])
        qkw = sb("qkw", [P, 2 * C, D])
        qT, kT = qkw[:, 0:C, :], qkw[:, C:2 * C, :]
        vr = sb("vr", [P, C, D])
        s01 = sb("s01", [P, 2 * C, D])
        s0, s1 = s01[:, 0:C, :], s01[:, C:2 * C, :]
        cnt = sb("cnt", [P, 2, C, N])
        adjT = sb("adjT", [P, C, N])
        wring = sb("wring", [P, WSLOTS, C, D])
        bring = sb("bring", [P, BATCH, COLT, D])
        stage = sb("stage", [P, 2, BATCH, D])
        rring = sb("rring", [P, RSLOTS, D])
        colsb = sb("colsb", [P, NCOLS])
        alph = sb("alph", [P, 2])
        attw = sb("attw", [P, 2, 32])
        ident = sb("ident", [P, P])
        bq8 = sb("bq8", [P, C])
        stat = sb("stat", [P, 8, C, 12])
        gcn_s = sb("gcn_s", [P, C, 8])
        gate = sb("gate", [P, 2, C, RELS])
        softmax_tmp = sb("softmax_tmp", [P, C, N // 2])

        edge_i = sb("edge_i", [P, 3, ECH], I32)
        dst_part = sb("dst_part", [P, 2, ECH], I32)
        edge_f = sb("edge_f", [P, 4, ECH])
        src_f, dst_lo, rel1, field = (edge_f[:, a, :] for a in range(4))
        edge_w = sb("edge_w", [P, ECH], I32)
        iota = sb("iota_row", [P, N], F16)
        ones = sb("ones", [P, 1])
        zeros = sb("zeros", [P, N], BF16)
        mask = sb("mask", [P, C, N], BF16)
        tally = sb("tally", [P, 4])
        flag = sb("flag", [1, 1], I32)
        hot_s = cnt[:, :, :, :].rearrange("p r c n -> p (r c n)").bitcast(BF16).rearrange("p (r n) -> p r n", r=HOT)
        hot_d = adjT[:, 0:2, :].rearrange("p a n -> p (a n)").bitcast(BF16).rearrange("p (r n) -> p r n", r=HOT)
        packed = adjT[:, 3, :].bitcast(I32)
        digits = s01[:, :, :].bitcast(I32)

        def col(name, i=0, n=1):
            at = COLS[name][0]
            return colsb[:, at + i:at + i + n]

        def row(name):
            return rring[:, ROWS.index(name) % RSLOTS, :]

        def weight(name):
            return wring[:, WEIGHTS.index(name) % WSLOTS, :, :]

        def need_row(eng, name):
            i = ROWS.index(name)
            eng.wait_ge(sem(f"row_slot{i % RSLOTS}_loaded"), 16 * (i // RSLOTS + 1))

        def need_weight(eng, name):
            i = WEIGHTS.index(name)
            eng.wait_ge(sem(f"weight_slot{i % WSLOTS}_loaded"), 16 * (i // WSLOTS + 1))

        def st(use, c, a, b=None):
            return stat[:, use, c, a:(a + 1 if b is None else b)]

        def norms(use, c):
            return 2 * C + 2 * c + use - 1 if use in (2, 3) else use * C + c + 1

        def blk(t, c):
            return slice(c * t, (c + 1) * t)

        with nc.Block() as block:

            @block.sync
            def _(sp):
                for i, e in enumerate((src, dst, etype)):
                    sp.dma_start(edge_i[:, i, :], e).then_inc(sem("edges_loaded"), 16)
                sp.dma_start(xr[:, :, :], x).then_inc(sem("x_loaded"), 16)
                sp.dma_start(colsb[:, :], cols).then_inc(sem("cols_loaded"), 16)
                sp.dma_start(alph[:, :], alphas.partition_broadcast(P)).then_inc(sem("cols_loaded"), 16)
                sp.wait_ge(sem("att_zero"), 1)
                for layer in range(2):
                    for c in range(C):
                        for r in range(RELS):
                            q = r * C + c
                            sp.dma_start(attw[c * BASES:(c + 1) * BASES, layer, q:q + 1],
                                         att[layer, r, :].rearrange("(b a) -> b a", a=1)).then_inc(
                                             sem("att_loaded"), 16)
                for n in range(2 * UNITS + BATCH):
                    if n < 2 * UNITS:
                        if n >= BATCH:
                            sp.wait_ge(sem("basis_used"), n - BATCH + 1)
                        sp.dma_start(bring[0:KB, n % BATCH, :, :], basis[n]).then_inc(
                            sem(f"basis{n % BATCH}_loaded"), 16)
                    if n % BATCH == BATCH - 1 and n >= 2 * BATCH - 1:
                        b = n // BATCH - 1
                        sp.wait_ge(sem("stage_ready"), (b + 1) * BATCH)
                        layer, g = divmod(b, BATCHES)
                        for j in range(COLT):
                            at = j * UNITS + g * BATCH
                            sp.dma_start(scratch[layer, at:at + BATCH, :, :].rearrange("g q o -> q g o"),
                                         stage[32 * j:32 * j + Q, b % 2, :, :]).then_inc(sem(f"w_stored{b % 2}"), 16)
                for c in range(C):
                    sp.wait_ge(sem("rel1_out_sum"), c + 1)
                    sp.dma_start(out[:, c, :], hr[:, c, :]).then_inc(sem("out_stored"), 16)
                sp.wait_ge(sem("out_stored"), 16 * C)

            @block.gpsimd
            def _(pool):
                pool.memset(attw[:, :, :], 0.0).then_inc(sem("att_zero"), 1)
                pool.iota(iota[:, :], [[1, N]], base=0, channel_multiplier=0,
                          allow_small_or_imprecise_dtypes=True).then_inc(sem("iota"), 1)
                pool.memset(zeros[:, :], 0.0).then_inc(sem("zeros"), 1)
                pool.memset(ones[:, :], 1.0).then_inc(sem("ones"), 1)
                pool.memset(ident[:, :], 0.0).then_inc(sem("ident0"), 1)
                pool.wait_ge(sem("ident0"), 1)
                pool.affine_select(out=ident[:, :], in_=ident[:, :], compare_op=ALU.not_equal, fill=1.0,
                                   base=0, pattern=[[-1, P]], channel_multiplier=1).then_inc(sem("ident"), 1)

                for i in range(WSLOTS):
                    pool.dma_start(weight(WEIGHTS[i]), weights[i]).then_inc(sem(f"weight_slot{i}_loaded"), 16)
                for i in range(RSLOTS):
                    pool.dma_start(row(ROWS[i]), rows[i, :].partition_broadcast(P)).then_inc(
                        sem(f"row_slot{i}_loaded"), 16)

                def load_weight(name):
                    i = WEIGHTS.index(name)
                    last, tiles = LAST_READ[WEIGHTS[i - WSLOTS]]
                    pool.wait_ge(sem(last), tiles)
                    pool.dma_start(weight(name), weights[i]).then_inc(sem(f"weight_slot{i % WSLOTS}_loaded"), 16)

                def load_row(name, last):
                    i = ROWS.index(name)
                    pool.wait_ge(sem(last), C)
                    pool.dma_start(row(name), rows[i, :].partition_broadcast(P)).then_inc(
                        sem(f"row_slot{i % RSLOTS}_loaded"), 16)

                def load_w(layer):
                    for par in range(2):
                        pool.wait_ge(sem(f"w_stored{par}"), (layer + 1) * (BATCHES // 2) * COLT * 16)
                    pool.wait_ge(sem("rel0_out" if layer else "adjT_psum"), C)
                    pool.dma_start(qkw[:, :, :], scratch[layer]).then_inc(sem("w_loaded"), 16)

                for n in ("f1a", "f1b", "f2a"):
                    load_weight(n)
                load_row("be2", "v")
                load_row("lin_b", "h_plus_bo")
                load_weight("f2b")
                load_row("lin_a", "h1")
                load_row("gcn_b", "h1")
                load_row("bias1", "h1_plus_b2")
                load_weight("lin")
                load_w(0)
                load_weight("c1_0")
                load_weight("c2_0")
                load_weight("c1_1")
                load_row("bias2", "x1")
                for n in ("c2_1", "gcn", "root1", "root2"):
                    load_weight(n)
                load_w(1)

            @block.scalar
            def _(act):
                def root(use, c):
                    act.wait_ge(sem("var_inverse"), norms(use, c))
                    act.activation(st(use, c, 9), st(use, c, 8), ACT.Sqrt).then_inc(sem("rstd"), 1)

                def relu_norm(use, c, done):
                    root(use, c)
                    act.wait_ge(sem(f"nbias{use}"), c + 1)
                    act.activation(hr[:, c, :], xr[:, c, :], ACT.Relu, scale=st(use, c, 9),
                                   bias=st(use, c, 10)).then_inc(sem(done), 1)

                def turn(done, dest, c):
                    act.wait_ge(sem(done + "_psum"), c + 1)
                    act.copy(dest[:, :, blk(P, c)],
                             bank[4 + c % 2][:, :].rearrange("p (f n) -> p f n", f=C)).then_inc(sem(done), 1)

                def take(done, dest, c, bias=0.0, func=ACT.Identity, b=None):
                    act.wait_ge(sem(done + "_psum"), c + 1)
                    act.activation(dest, bank[c % C][:, :], func, bias=bias).then_inc(sem(b or done), 1)

                def stage_units(first, n):
                    for u in range(first, first + n):
                        b = u // BATCH
                        act.wait_ge(sem("basis_used"), u + 1)
                        if b >= 2 and u % BATCH == 0:
                            act.wait_ge(sem(f"w_stored{b % 2}"), (b // 2) * COLT * 16)
                        act.copy(stage[:, b % 2, u % BATCH, :], bank[6 + u % 2][:, :]).then_inc(
                            sem("stage_ready"), 1)

                for c in range(C):
                    relu_norm(0, c, "h0")
                for c in range(C):
                    turn("hT0", hT, c)
                act.wait_ge(sem("cols_loaded"), 32)
                act.wait_ge(sem("bq8"), 1)
                for c in range(C):
                    act.wait_ge(sem("q_psum"), c + 1)
                    act.activation(qT[:, c, :], bank[c][:, :], ACT.Identity, scale=HD ** -0.5,
                                   bias=bq8[:, c:c + 1]).then_inc(sem("q"), 1)
                for c in range(C):
                    take("k", kT[:, c, :], c, col("bk", c))
                act.wait_ge(sem("digits"), C)
                act.activation(cnt[:, 0, :, :], digits[:, 0:C, :], ACT.Copy,
                               accum_out=tally[:, 0:1]).then_inc(sem("counts0"), 1)
                for it in range(2 * C):
                    act.wait_ge(sem("centred"), it + 1)
                    sc = s01[:, (it % 2) * C:(it % 2 + 1) * C, :]
                    act.activation(sc, sc, ACT.Exp).then_inc(sem("exped"), 1)
                    stage_units(it * BATCH, BATCH)
                act.wait_ge(sem("pv_used"), 2 * C)
                for c in range(C):
                    act.copy(s0[:, c, :], bank[c][:, :]).then_inc(sem("ao"), 1)
                root(1, 0)
                root(1, 1)
                stage_units(32, 2)
                root(1, 2)
                root(1, 3)
                stage_units(34, 2)
                for c in range(C):
                    turn("h1T", hT, c)
                for t in range(2 * C):
                    take("ff1", s01[:, t, :], t, col("b1", t), ACT.Relu)
                stage_units(36, 2)
                for c in range(C):
                    root(2, c)
                    relu_norm(3, c, "h2")
                    if c == 1:
                        turn("hT2", hT, 0)
                        turn("hT2", hT, 1)
                stage_units(38, 2)
                turn("hT2", hT, 2)
                turn("hT2", hT, 3)
                def batch_norm(l, c):
                    root(4 + l, c)
                    act.wait_ge(sem(f"bnb{l}"), c + 1)
                    act.activation(s1[:, c, :], s1[:, c, :], ACT.Relu, scale=st(4 + l, c, 10),
                                   bias=st(4 + l, c, 11)).then_inc(sem(f"bn{l}"), 1)

                for c in range(C):
                    take("agg0", hT[:, c, :], c)
                for l in range(2):
                    for c in range(C):
                        take(f"c1_{l}", s0[:, c, :], c, col("c1b", l * C + c), b=f"c1_{l}_sum")
                    take(f"c2_{l}", s1[:, 0, :], 0, col("c2b", l * C))
                    take(f"c2_{l}", s1[:, 1, :], 1, col("c2b", l * C + 1))
                    batch_norm(l, 0)
                    batch_norm(l, 1)
                    take(f"c2_{l}", s1[:, 2, :], 2, col("c2b", l * C + 2))
                    take(f"c2_{l}", s1[:, 3, :], 3, col("c2b", l * C + 3))
                    if l == 0:
                        stage_units(40, 2)
                        batch_norm(0, 2)
                        turn("x3", vr, 0)
                        batch_norm(0, 3)
                        turn("x3", vr, 1)
                        take("agg1", hT[:, 0, :], 0)
                        turn("x3", vr, 2)
                        take("agg1", hT[:, 1, :], 1)
                        turn("x3", vr, 3)
                        take("agg1", hT[:, 2, :], 2)
                        take("agg1", hT[:, 3, :], 3)
                        stage_units(42, 2)
                    else:
                        stage_units(44, 1)
                        batch_norm(1, 2)
                        stage_units(45, 1)
                        batch_norm(1, 3)
                        stage_units(46, 4)
                act.wait_ge(sem("deg"), 1)
                act.activation(gcn_s[:, :, 2], gcn_s[:, :, 1], ACT.Sqrt).then_inc(sem("dinv"), 1)
                for c in range(C):
                    root(6, c)
                    act.wait_ge(sem("gcn_nb"), c + 1)
                    act.activation(hr[:, c, :], xr[:, c, :], ACT.Relu, scale=gcn_s[:, c, 3:4],
                                   bias=gcn_s[:, c, 4:5]).then_inc(sem("h_gcn"), 1)
                    if c == 1:
                        stage_units(50, 2)
                for c in range(C):
                    take("agg2", hT[:, c, :], c)
                stage_units(52, 2)
                def gates(layer, c):
                    act.wait_ge(sem(f"gates{layer}"), c + 1)
                    act.activation(gate[:, layer, c, :], bank[4 + c % 2][:, 0:RELS], ACT.Sigmoid).then_inc(
                        sem(f"sigmoid{layer}"), 1)

                def gated1(layer, c):
                    act.wait_ge(sem(f"sigmoid{layer}"), c + 1)
                    act.activation(s1[:, c, :], hr[:, c, :], ACT.Copy,
                                   scale=gate[:, layer, c, 1:2]).then_inc(sem(f"gated1_{layer}"), 1)

                def G0(layer):
                    for c in range(C):
                        act.wait_ge(sem(f"G0_{layer}_psum"), c + 1)
                        act.copy(vr[:, c, :], bank[c][:, :]).then_inc(sem(f"G0_{layer}"), 1)

                relu_norm(7, 0, "h_rel0")
                relu_norm(7, 1, "h_rel0")
                stage_units(54, 2)
                turn("relT0", hT, 0)
                turn("relT0", hT, 1)
                stage_units(56, 2)
                relu_norm(7, 2, "h_rel0")
                stage_units(58, 2)
                relu_norm(7, 3, "h_rel0")
                gates(0, 0)
                gates(0, 1)
                gated1(0, 0)
                gated1(0, 1)
                stage_units(60, 2)
                turn("relT0", hT, 2)
                turn("relT0", hT, 3)
                stage_units(62, 2)
                gates(0, 2)
                gates(0, 3)
                gated1(0, 2)
                gated1(0, 3)
                G0(0)
                for c in range(C):
                    turn("relT1", hT, c)
                    gates(1, c)
                    gated1(1, c)
                G0(1)

            @block.vector
            def _(dve):
                steps = [0]

                def step(ins):
                    steps[0] += 1
                    ins.then_inc(sem("dve_step"), 1)
                    return steps[0]

                def after(n):
                    dve.wait_ge(sem("dve_step"), n)

                dve.wait_ge(sem("edges_loaded"), 48)
                dve.tensor_copy(src_f, edge_i[:, 0, :]).then_inc(sem("edge_step"), 1)
                dve.tensor_scalar(dst_part[:, 0, :], edge_i[:, 1, :], P - 1, None, ALU.bitwise_and).then_inc(
                    sem("edge_step"), 1)
                dve.tensor_scalar(dst_part[:, 1, :], edge_i[:, 1, :], P.bit_length() - 1, None,
                                  ALU.logical_shift_right).then_inc(sem("edge_step"), 1)
                dve.tensor_scalar(rel1, edge_i[:, 2, :], 0.0, None, ALU.not_equal).then_inc(sem("edge_step"), 1)
                dve.wait_ge(sem("edge_step"), 4)
                dve.tensor_copy(dst_lo, dst_part[:, 0, :]).then_inc(sem("edge_step"), 1)
                dve.scalar_tensor_tensor(field, rel1, float(C), dst_part[:, 1, :], ALU.mult, ALU.add).then_inc(
                    sem("edge_step"), 1)
                dve.wait_ge(sem("edge_step"), 6)
                dve.tensor_scalar(edge_w[:, :], field, -FBITS * 2.0 ** 23, 127 * 2.0 ** 23, ALU.mult,
                                  ALU.add).then_inc(sem("edge_step"), 1)
                dve.wait_ge(sem("edge_step"), 7)
                dve.wait_ge(sem("iota"), 1)
                weight_f = edge_w[:, :].bitcast(F32)

                def one_hots(n):
                    if n >= HOT:
                        dve.wait_ge(sem("hot_used"), n - HOT + 1)
                    dve.tensor_scalar(hot_d[:, n % HOT, :], iota[:, 0:P], dst_lo[:, n:n + 1],
                                      weight_f[:, n:n + 1], ALU.is_equal, ALU.mult).then_inc(sem("hot_ready"), 1)
                    dve.tensor_scalar(hot_s[:, n % HOT, :], iota[:, :], src_f[:, n:n + 1], None,
                                      ALU.is_equal).then_inc(sem("hot_ready"), 1)

                def norm_stats(use, t, c, width=1):
                    dve.bn_stats(st(use, c, 0, 6), t).then_inc(sem("dve_step"), 1)
                    steps[0] += 1
                    after(steps[0])
                    after(step(dve.bn_aggr(st(use, c, 6, 8), st(use, c, 0, 6))))
                    after(step(dve.tensor_scalar(st(use, c, 7), st(use, c, 7), LN_EPS, None, ALU.add)))
                    dve.reciprocal(st(use, c, 8), st(use, c, 7)).then_inc(sem("var_inverse"), 1)

                def nbias(use, c):
                    dve.wait_ge(sem("rstd"), norms(use, c))
                    dve.tensor_scalar(st(use, c, 10), st(use, c, 6), st(use, c, 9), -1.0, ALU.mult,
                                      ALU.mult).then_inc(sem(f"nbias{use}"), 1)

                def relu_norm_stats(use, ready):
                    for c in range(C):
                        if ready:
                            dve.wait_ge(sem(ready), c + 1)
                        norm_stats(use, xr[:, c, :], c)
                        nbias(use, c)

                dve.wait_ge(sem("cols_loaded"), 32)
                dve.tensor_scalar(bq8[:, :], col("bq", 0, C), HD ** -0.5, None, ALU.mult).then_inc(sem("bq8"), 1)
                for n in range(ECH):
                    one_hots(n)
                    if n == HOT - 1:
                        dve.wait_ge(sem("x_loaded"), 16)
                        relu_norm_stats(0, None)
                dve.wait_ge(sem("hot_used"), ECH)
                dve.tensor_scalar(packed, bank[7][:, :], 2.0 ** UNIT_BITS, None, ALU.mult).then_inc(
                    sem("packed"), 1)
                dve.reduce_max(tally[:, 2:3], bank[7][:, :], axis=mybir.AxisListType.X).then_inc(sem("packed"), 1)
                dve.wait_ge(sem("packed"), 2)
                for f in range(FIELDS):
                    dve.tensor_scalar(digits[:, f, :], packed, FBITS * (FIELDS - 1 - f), 2 ** FBITS - 1,
                                      ALU.logical_shift_right, ALU.bitwise_and).then_inc(sem("digits"), 1)
                dve.wait_ge(sem("digits"), FIELDS)
                dve.tensor_scalar(cnt[:, 1, :, :], digits[:, C:2 * C, :], 0.0, 0.0, ALU.add, ALU.add,
                                  accum_out=tally[:, 1:2]).then_inc(sem("counts1"), 1)
                dve.tensor_scalar(tally[:, 3:4], tally[:, 2:3], 2.0 ** FBITS, TOO_MANY, ALU.is_ge,
                                  ALU.mult).then_inc(sem("tally_step"), 1)
                dve.wait_ge(sem("counts0"), 1)
                dve.wait_ge(sem("counts1"), 1)
                dve.wait_ge(sem("tally_step"), 1)
                dve.scalar_tensor_tensor(tally[:, 3:4], tally[:, 3:4], tally[:, 0:1], tally[:, 1:2], ALU.add,
                                         ALU.add).then_inc(sem("tally"), 1)
                need_row(dve, "bv")
                for c in range(C):
                    dve.wait_ge(sem("v_psum"), c + 1)
                    dve.tensor_tensor(vr[:, c, :], bank[c][:, :], row("bv"), ALU.add).then_inc(sem("v"), 1)
                dve.wait_ge(sem("tally_sum"), 1)
                dve.tensor_scalar(flag[:, :], bank[6][0:1, 0:1], float(EDGES), None, ALU.is_equal).then_inc(
                    sem("flag"), 1)
                dve.wait_ge(sem("flag"), 1)
                fits = dve.value_load(flag[0:1, 0:1])
                with dve.If(fits < 1):
                    slow_d = s0[:, 0, 0:N // 2].bitcast(BF16)
                    slow_s = s0[:, 1, 0:N // 2].bitcast(BF16)
                    dst_f, rel_f = field, dst_lo
                    dve.tensor_copy(dst_f, edge_i[:, 1, :]).then_inc(sem("slow_step"), 1)
                    for r in range(RELS):
                        dve.tensor_scalar(rel_f, rel1, float(r), None, ALU.is_equal).then_inc(sem("slow_step"), 1)
                        dve.wait_ge(sem("slow_step"), r + 2)
                        with dve.Fori(0, ECH) as n:
                            dve.wait_ge(sem("slow_used"), n + (r * (ECH + 1) + 1))
                            dve.tensor_scalar(slow_d, iota[:, :], dst_f[:, bass.ds(n, 1)], None,
                                              ALU.is_equal).then_inc(sem("slow_hot"), 1)
                            dve.tensor_scalar(slow_s, iota[:, :], src_f[:, bass.ds(n, 1)],
                                              rel_f[:, bass.ds(n, 1)], ALU.is_equal, ALU.mult).then_inc(
                                                  sem("slow_hot"), 1)
                        dve.wait_ge(sem("slow_counted"), r + 1)
                        for c in range(C):
                            dve.tensor_copy(cnt[:, r, c, :], bank[c][:, :]).then_inc(sem("slow_copied"), 1)
                    dve.wait_ge(sem("slow_copied"), RELS * C)
                for c in range(C):
                    dve.tensor_tensor(mask[:, c, :], cnt[:, 0, c, :], cnt[:, 1, c, :], ALU.logical_or).then_inc(
                        sem("mask"), 1)
                NH = N // 2
                tmp = softmax_tmp

                def scores_of(it):
                    return s01[:, (it % 2) * C:(it % 2 + 1) * C, :].rearrange("p c (a n) -> p (c a) n", a=2)

                def take_scores(it):
                    half_n, m = divmod(it, C)
                    if it >= 2:
                        dve.wait_ge(sem("pv_used"), it - 1)
                    dve.wait_ge(sem("mask"), m + 1)
                    for q in range(4):
                        h0 = 4 * (q // 2) + q % 2
                        dve.wait_ge(sem("scores_psum"), it * 4 + q + 1)
                        dve.tensor_tensor(scores_of(it)[:, h0:h0 + 3:2, :],
                                          bank[4 + q % 2][:, :].rearrange("p (a n) -> p a n", a=2),
                                          mask[:, m, blk(NH, half_n)].unsqueeze(1).to_broadcast([P, 2, NH]),
                                          ALU.mult).then_inc(sem("scores"), 1)

                take_scores(0)
                need_row(dve, "bo")
                for it in range(2 * C):
                    sc = scores_of(it)
                    dve.wait_ge(sem("scores"), 4 * it + 4)
                    if it:
                        dve.wait_ge(sem("probs"), it)
                    after(step(dve.tensor_tensor(tmp[:, 0:4, :], sc[:, 0:4, :], sc[:, 4:8, :], ALU.max)))
                    after(step(dve.tensor_tensor(tmp[:, 0:2, :], tmp[:, 0:2, :], tmp[:, 2:4, :], ALU.max)))
                    after(step(dve.tensor_tensor(tmp[:, 0, :], tmp[:, 0, :], tmp[:, 1, :], ALU.max)))
                    dve.tensor_tensor(sc, sc, tmp[:, 0:1, :].to_broadcast([P, HEADS, NH]),
                                      ALU.subtract).then_inc(sem("centred"), 1)
                    if it + 1 < 2 * C:
                        take_scores(it + 1)
                    else:
                        for c in range(C):
                            dve.wait_ge(sem("hT0_psum"), c + 1)
                            dve.tensor_tensor(hr[:, c, :], hr[:, c, :], row("bo"), ALU.add).then_inc(
                                sem("h_plus_bo"), 1)
                    dve.wait_ge(sem("exped"), it + 1)
                    after(step(dve.tensor_tensor(tmp[:, 0:4, :], sc[:, 0:4, :], sc[:, 4:8, :], ALU.add)))
                    after(step(dve.tensor_tensor(tmp[:, 0:2, :], tmp[:, 0:2, :], tmp[:, 2:4, :], ALU.add)))
                    after(step(dve.tensor_tensor(tmp[:, 0, :], tmp[:, 0, :], tmp[:, 1, :], ALU.add)))
                    after(step(dve.reciprocal(tmp[:, 1, :], tmp[:, 0, :])))
                    dve.tensor_tensor(sc, sc, tmp[:, 1:2, :].to_broadcast([P, HEADS, NH]),
                                      ALU.mult).then_inc(sem("probs"), 1)

                def affine_norm(use, t, c, g, be, dest, done):
                    dve.wait_ge(sem("var_inverse"), norms(use, c))
                    after(step(dve.scalar_tensor_tensor(t, t, st(use, c, 6), row(g), ALU.subtract, ALU.mult)))
                    dve.wait_ge(sem("rstd"), norms(use, c))
                    dve.scalar_tensor_tensor(dest, t, st(use, c, 9), be, ALU.mult, ALU.add).then_inc(sem(done), 1)

                for n in ("g1", "be1", "b2", "g2"):
                    need_row(dve, n)
                for c in range(C):
                    dve.wait_ge(sem("o_psum"), c + 1)
                    dve.wait_ge(sem("h_plus_bo"), c + 1)
                    after(step(dve.tensor_tensor(vr[:, c, :], bank[c][:, :], hr[:, c, :], ALU.add)))
                    norm_stats(1, vr[:, c, :], c)
                    affine_norm(1, vr[:, c, :], c, "g1", row("be1"), vr[:, c, :], "h1")
                dve.wait_ge(sem("ident"), 1)
                for c in range(C):
                    after(step(dve.tensor_tensor(qT[:, c, :], cnt[:, 0, c, :], cnt[:, 1, c, :], ALU.add)))
                    dve.tensor_tensor(qT[:, c, blk(P, c)], qT[:, c, blk(P, c)], ident[:, :],
                                      ALU.add).then_inc(sem("adj"), 1)
                for c in range(C):
                    dve.wait_ge(sem("h1T_psum"), c + 1)
                    dve.tensor_tensor(vr[:, c, :], vr[:, c, :], row("b2"), ALU.add).then_inc(sem("h1_plus_b2"), 1)
                for c in range(C):
                    dve.wait_ge(sem("adj"), c + 1)
                    n = step(dve.reduce_sum(gcn_s[:, c, 0:1], qT[:, c, :], axis=mybir.AxisListType.X))
                after(n)
                dve.reciprocal(gcn_s[:, :, 1], gcn_s[:, :, 0]).then_inc(sem("deg"), 1)
                need_row(dve, "be2")
                for c in range(C):
                    dve.wait_ge(sem("h0"), c + 1)
                    dve.tensor_tensor(xr[:, c, :], xr[:, c, :], row("be2"), ALU.add).then_inc(sem("x_plus"), 1)
                for c in range(C):
                    dve.wait_ge(sem("adjT_psum"), c + 1)
                    dve.tensor_copy(adjT[:, :, blk(P, c)],
                                    bank[4 + c % 2][:, :].rearrange("p (f n) -> p f n", f=C)).then_inc(
                                        sem("adjT"), 1)
                for c in range(C):
                    dve.wait_ge(sem("ff2_psum"), c + 1)
                    dve.wait_ge(sem("h1_plus_b2"), c + 1)
                    after(step(dve.tensor_tensor(hr[:, c, :], bank[c][:, :], vr[:, c, :], ALU.add)))
                    norm_stats(2, hr[:, c, :], c)
                    dve.wait_ge(sem("x_plus"), c + 1)
                    affine_norm(2, hr[:, c, :], c, "g2", xr[:, c, :], xr[:, c, :], "x1")
                    dve.wait_ge(sem("x1"), c + 1)
                    norm_stats(3, xr[:, c, :], c)
                    nbias(3, c)
                need_row(dve, "lin_b")
                need_row(dve, "lin_a")
                for c in range(C):
                    dve.wait_ge(sem("lin_psum"), c + 1)
                    after(step(dve.tensor_tensor(s1[:, c, :], bank[c][:, :], row("lin_b"), ALU.add)))
                    after(step(dve.scalar_tensor_tensor(s0[:, c, :], s1[:, c, :], 0.0, row("lin_a"),
                                                        ALU.min, ALU.mult)))
                    dve.scalar_tensor_tensor(vr[:, c, :], s1[:, c, :], 0.0, s0[:, c, :], ALU.max,
                                             ALU.add).then_inc(sem("x2"), 1)
                for l in range(2):
                    for c in range(C):
                        dve.wait_ge(sem(f"c1_{l}_sum"), c + 1)
                        after(step(dve.tensor_scalar(vr[:, c, :], s0[:, c, :], 0.0, alph[:, l:l + 1], ALU.min,
                                                     ALU.mult)))
                        dve.scalar_tensor_tensor(s0[:, c, :], s0[:, c, :], 0.0, vr[:, c, :], ALU.max,
                                                 ALU.add).then_inc(sem(f"c1_{l}"), 1)
                    for c in range(C):
                        dve.wait_ge(sem(f"c2_{l}"), c + 1)
                        norm_stats(4 + l, s1[:, c, :], c)
                        dve.wait_ge(sem("rstd"), norms(4 + l, c))
                        after(step(dve.tensor_scalar(st(4 + l, c, 10), st(4 + l, c, 9), col("gam", l * C + c), None,
                                                     ALU.mult)))
                        after(step(dve.tensor_scalar(st(4 + l, c, 11), st(4 + l, c, 6), st(4 + l, c, 10), -1.0,
                                                     ALU.mult, ALU.mult)))
                        dve.tensor_scalar(st(4 + l, c, 11), st(4 + l, c, 11), col("bet", l * C + c), None,
                                          ALU.add).then_inc(sem(f"bnb{l}"), 1)
                for c in range(C):
                    dve.wait_ge(sem("x4_psum"), c + 1)
                    dve.tensor_tensor(xr[:, c, :], xr[:, c, :], bank[4 + c % 2][:, :], ALU.add).then_inc(
                        sem("x5"), 1)
                    dve.wait_ge(sem("x5"), c + 1)
                    norm_stats(6, xr[:, c, :], c)
                    dve.wait_ge(sem("dinv"), 1)
                    dve.wait_ge(sem("rstd"), norms(6, c))
                    after(step(dve.tensor_scalar(gcn_s[:, c, 3:4], st(6, c, 9), gcn_s[:, c, 2:3], None, ALU.mult)))
                    dve.tensor_scalar(gcn_s[:, c, 4:5], st(6, c, 6), gcn_s[:, c, 3:4], -1.0, ALU.mult,
                                      ALU.mult).then_inc(sem("gcn_nb"), 1)
                need_row(dve, "gcn_b")
                for c in range(C):
                    dve.wait_ge(sem("gcn_psum"), c + 1)
                    after(step(dve.scalar_tensor_tensor(s0[:, c, :], bank[c][:, :], gcn_s[:, c, 2:3], row("gcn_b"),
                                                        ALU.mult, ALU.add)))
                    after(step(dve.scalar_tensor_tensor(s1[:, c, :], s0[:, c, :], 0.01, s0[:, c, :], ALU.mult,
                                                        ALU.max)))
                    dve.wait_ge(sem("h_gcn"), c + 1)
                    dve.tensor_tensor(xr[:, c, :], xr[:, c, :], s1[:, c, :], ALU.add).then_inc(sem("x6"), 1)
                    dve.wait_ge(sem("x6"), c + 1)
                    norm_stats(7, xr[:, c, :], c)
                    nbias(7, c)
                need_row(dve, "bias1")
                need_row(dve, "bias2")

                def gated0(layer, c):
                    dve.wait_ge(sem(f"sigmoid{layer}"), c + 1)
                    dve.tensor_scalar(s0[:, c, :], hr[:, c, :], gate[:, layer, c, 0:1], None,
                                      ALU.mult).then_inc(sem(f"gated0_{layer}"), 1)

                def G1(layer):
                    for c in range(C):
                        dve.wait_ge(sem(f"G1_{layer}_psum"), c + 1)
                        dve.tensor_copy(adjT[:, c, :], bank[c][:, :]).then_inc(sem(f"G1_{layer}"), 1)

                for c in range(C):
                    gated0(0, c)
                for c in range(C):
                    dve.wait_ge(sem("h_rel0"), c + 1)
                    dve.tensor_tensor(xr[:, c, :], xr[:, c, :], row("bias2"), ALU.add).then_inc(
                        sem("x_plus_bias2"), 1)
                G1(0)
                dve.wait_ge(sem("gated1_0"), C)
                dve.wait_ge(sem("gated0_0"), C)
                for c in range(C):
                    dve.wait_ge(sem("rel0_psum"), c + 1)
                    after(step(dve.tensor_tensor(hr[:, c, :], bank[c][:, :], row("bias1"), ALU.add)))
                    dve.tensor_scalar(hr[:, c, :], hr[:, c, :], 0.0, None, ALU.max).then_inc(sem("rel0_out"), 1)
                    if c:
                        gated0(1, c - 1)
                gated0(1, C - 1)
                G1(1)
                dve.wait_ge(sem("gated1_1"), C)
                dve.wait_ge(sem("gated0_1"), C)
                dve.wait_ge(sem("x_plus_bias2"), C)
                for c in range(C):
                    dve.wait_ge(sem("rel1_psum"), c + 1)
                    dve.tensor_tensor(hr[:, c, :], bank[c][:, :], xr[:, c, :], ALU.add).then_inc(
                        sem("rel1_out_sum"), 1)

            @block.tensor
            def _(pe):
                def turn(src, c, ready, done, free=None):
                    pe.wait_ge(sem(ready), c + 1)
                    if c >= 2:
                        pe.wait_ge(sem(done), c - 1)
                    elif free:
                        pe.wait_ge(sem(free), C)
                    for f in range(C):
                        mm = pe.transpose(bank[4 + c % 2][:, blk(P, f)], src[:, c, blk(P, f)], ident[:, :])
                    mm.then_inc(sem(done + "_psum"), 1)

                def units(first, n):
                    for u in range(first, first + n):
                        if u == 0:
                            pe.wait_ge(sem("att_loaded"), 16 * 2 * Q)
                        if u >= 2:
                            pe.wait_ge(sem("stage_ready"), u - 1)
                        pe.wait_ge(sem(f"basis{u % BATCH}_loaded"), 16 * (u // BATCH + 1))
                        for j in range(COLT):
                            mm = pe.matmul(bank[6 + u % 2][32 * j:32 * j + 32, :], attw[0:KB, u // UNITS, :],
                                           bring[0:KB, u % BATCH, j, :], start=True, stop=True,
                                           tile_position=(0, 32 * j))
                        mm.then_inc(sem("basis_used"), 1)

                IN_PAIRS = [(c, k) for pair in ((0, 1), (2, 3)) for k in range(C) for c in pair]
                BY_TILE = [(c, k) for c in range(C) for k in range(C)]
                ALL_BANKS = [(c, k) for k in range(C) for c in range(C)]

                def products(lhs, rhs, ready, done, order=IN_PAIRS, kn=C, cs=range(C), t0=0):
                    seen = 0
                    for c, k in order:
                        if c not in cs:
                            continue
                        need = max(k, c) + 1
                        if ready and need > seen:
                            pe.wait_ge(sem(ready), need + t0)
                            seen = need
                        mm = pe.matmul(bank[c][:, :], lhs(k, c), rhs(k, c), start=(k == 0), stop=(k == kn - 1))
                        if k == kn - 1:
                            mm.then_inc(sem(done), 1)

                def stage_T(wname, rhs, ready, done, **kw):
                    need_weight(pe, wname)
                    w = weight(wname)
                    products(lambda k, c: w[:, k, blk(P, c)], lambda k, c: rhs[:, k, :], ready, done, **kw)

                def stage_row(wname, lhs, ready, done, **kw):
                    need_weight(pe, wname)
                    w = weight(wname)
                    products(lambda k, c: lhs[:, k, blk(P, c)], lambda k, c: w[:, k, :], ready, done, **kw)

                def aggregate(lhs, over, ready, done, **kw):
                    products(lambda k, c: lhs[:, k, blk(P, c)], lambda k, c: over[:, k, :], ready, done, **kw)

                def count(n):
                    pe.wait_ge(sem("hot_ready"), 2 * n + 2)
                    pe.matmul(bank[7][:, :], hot_d[:, n % HOT, :], hot_s[:, n % HOT, :], start=(n == 0),
                              stop=(n == ECH - 1)).then_inc(sem("hot_used"), 1)

                def qkv_tile(t):
                    which, c = divmod(t, C)
                    w = weight("qkv"[which])
                    if c == 0:
                        need_weight(pe, "qkv"[which])
                    if which:
                        pe.wait_ge(sem("qkv"[which - 1]), c + 1)
                    for k in range(C):
                        a, b = ((w[:, k, blk(P, c)], hT[:, k, :]) if which < 2 else
                                (hT[:, k, blk(P, c)], w[:, k, :]))
                        mm = pe.matmul(bank[c][:, :], a, b, start=(k == 0), stop=(k == C - 1))
                    mm.then_inc(sem("qkv"[which] + "_psum"), 1)

                first, every = FIRST_TILE, TILE_EVERY
                pe.wait_ge(sem("ident"), 1)
                for n in range(ECH):
                    count(n)
                    if first - 6 <= n < first - 2:
                        turn(hr, n - first + 6, "h0", "hT0")
                    if n == first:
                        pe.wait_ge(sem("hT0"), C)
                    if n >= first and (n - first) % every == 0 and (n - first) // every < 2 * C:
                        qkv_tile((n - first) // every)
                for t in range((ECH - 1 - first) // every + 1, 2 * C):
                    qkv_tile(t)
                for t in range(2 * C, 3 * C):
                    qkv_tile(t)
                pe.wait_ge(sem("tally"), 1)
                pe.wait_ge(sem("ones"), 1)
                pe.matmul(bank[6][0:1, 0:1], tally[:, 3:4], ones[:, :], start=True, stop=True).then_inc(
                    sem("tally_sum"), 1)
                pe.wait_ge(sem("flag"), 1)
                fits = pe.value_load(flag[0:1, 0:1])
                with pe.If(fits < 1):
                    slow_d = s0[:, 0, 0:N // 2].bitcast(BF16)
                    slow_s = s0[:, 1, 0:N // 2].bitcast(BF16)
                    pe.wait_ge(sem("v"), C)
                    pe.wait_ge(sem("zeros"), 1)
                    for r in range(RELS):
                        if r:
                            pe.wait_ge(sem("slow_copied"), C)
                        for c in range(C):
                            mm = pe.matmul(bank[c][:, :], zeros[:, 0:P], zeros[:, :], start=True, stop=False)
                        mm.then_inc(sem("slow_used"), 1)
                        with pe.Fori(0, ECH) as n:
                            pe.wait_ge(sem("slow_hot"), n * 2 + (2 * ECH * r + 2))
                            for c in range(C):
                                mm = pe.matmul(bank[c][:, :], slow_d[:, blk(P, c)], slow_s, start=False, stop=False)
                            mm.then_inc(sem("slow_used"), 1)
                        for c in range(C):
                            mm = pe.matmul(bank[c][:, :], zeros[:, 0:P], zeros[:, :], start=False, stop=True)
                        mm.then_inc(sem("slow_counted"), 1)
                pe.wait_ge(sem("v"), C)
                NH = N // 2
                pe.wait_ge(sem("k"), C)
                pe.wait_ge(sem("cols_loaded"), 32)

                def scores(it):
                    half_n, m = divmod(it, C)
                    for q in range(4):
                        h0 = 4 * (q // 2) + q % 2
                        at = HD * (q % 2)
                        if it or q >= 2:
                            pe.wait_ge(sem("scores"), it * 4 + q - 1)
                        for a in range(2):
                            t = (h0 + 2 * a) // 2
                            mm = pe.matmul(bank[4 + q % 2][:, blk(NH, a)], kT[at:at + HD, t, blk(P, m)],
                                           qT[at:at + HD, t, blk(NH, half_n)], start=True, stop=True)
                        mm.then_inc(sem("scores_psum"), 1)

                scores(0)
                for it in range(2 * C):
                    if it + 1 < 2 * C:
                        scores(it + 1)
                    units(it * BATCH, BATCH)
                    half_n, m = divmod(it, C)
                    sc = s01[:, (it % 2) * C:(it % 2 + 1) * C, :].rearrange("p c (a n) -> p (c a) n", a=2)
                    pe.wait_ge(sem("probs"), it + 1)
                    for h in range(HEADS):
                        at = HD * (h % 2)
                        mm = pe.matmul(bank[h // 2][at:at + HD, blk(NH, half_n)], vr[:, m, blk(HD, h)],
                                       sc[:, h, :], start=(m == 0), stop=(m == C - 1), skip_group_check=True)
                    mm.then_inc(sem("pv_used"), 1)
                stage_row("o", s0, "ao", "o_psum")
                units(32, 4)
                for c in range(C):
                    turn(vr, c, "h1", "h1T", "scores")
                pe.wait_ge(sem("h1T"), C)
                stage_T("f1a", hT, None, "ff1_psum", order=BY_TILE)
                for c in range(C):
                    turn(qT, c, "adj", "adjT", "h1T")
                stage_T("f1b", hT, "ff1", "ff1_psum", order=BY_TILE)
                need_weight(pe, "f2a")
                need_weight(pe, "f2b")
                w_a, w_b = weight("f2a"), weight("f2b")
                for cs in ((0, 1), (2, 3)):
                    for k in range(2 * C):
                        for c in cs:
                            pe.wait_ge(sem("ff1"), max(k + 1, C + c + 1))
                            mm = pe.matmul(bank[c][:, :], s01[:, k, blk(P, c)],
                                           (w_a if k < C else w_b)[:, k % C, :],
                                           start=(k == 0), stop=(k == 2 * C - 1))
                            if k == 2 * C - 1:
                                mm.then_inc(sem("ff2_psum"), 1)
                    if cs == (0, 1):
                        units(36, 2)
                turn(hr, 0, "h2", "hT2", "adjT")
                turn(hr, 1, "h2", "hT2", "adjT")
                need_weight(pe, "lin")

                def lin_tile(c):
                    pe.wait_ge(sem("hT2"), c + 1)
                    pe.wait_ge(sem("x1"), c + 1)
                    for k in range(C):
                        mm = pe.matmul(bank[c][:, :], hT[:, k, blk(P, c)], weight("lin")[:, k, :],
                                       start=(k == 0), stop=(k == C - 1))
                    mm.then_inc(sem("lin_psum"), 1)

                lin_tile(0)
                lin_tile(1)
                units(38, 2)
                turn(hr, 2, "h2", "hT2")
                lin_tile(2)
                turn(hr, 3, "h2", "hT2")
                lin_tile(3)
                pe.wait_ge(sem("adjT"), C)
                aggregate(vr, adjT, "x2", "agg0_psum")
                stage_T("c1_0", hT, "agg0", "c1_0_psum")
                stage_T("c2_0", s0, "c1_0", "c2_0_psum")
                units(40, 2)
                for c in range(C):
                    turn(s1, c, "bn0", "x3", "hT2")
                    if c:
                        pe.wait_ge(sem("x3"), c)
                        aggregate(vr, adjT, None, "agg1_psum", order=BY_TILE, cs=(c - 1,))
                pe.wait_ge(sem("x3"), C)
                aggregate(vr, adjT, None, "agg1_psum", order=BY_TILE, cs=(C - 1,))
                units(42, 2)
                stage_T("c1_1", hT, "agg1", "c1_1_psum")
                stage_T("c2_1", s0, "c1_1", "c2_1_psum")
                units(44, 4)
                pe.wait_ge(sem("bn1"), C)
                pe.wait_ge(sem("x3"), C)
                for c in range(C):
                    if c >= 2:
                        pe.wait_ge(sem("x5"), c - 1)
                    for f in range(C):
                        mm = pe.transpose(bank[4 + c % 2][:, blk(P, f)], s1[:, f, blk(P, c)], ident[:, :])
                    mm.then_inc(sem("x4_psum"), 1)
                    if c == 1:
                        units(48, 2)
                units(50, 2)
                aggregate(hr, adjT, "h_gcn", "agg2_psum")
                units(52, 2)
                stage_row("gcn", hT, "agg2", "gcn_psum", cs=(0, 1))
                units(54, 2)
                stage_row("gcn", hT, "agg2", "gcn_psum", cs=(2, 3))
                def gates(layer, c):
                    pe.wait_ge(sem(f"relT{layer}"), c + 1)
                    for k in range(C):
                        mm = pe.matmul(bank[4 + c % 2][:, 0:RELS], hT[:, k, blk(P, c)],
                                       col(f"gw{layer + 1}", k * RELS, RELS), start=(k == 0), stop=(k == C - 1))
                    mm.then_inc(sem(f"gates{layer}"), 1)

                def G(layer, r, ks):
                    g = (s0, s1)[r]
                    for k in ks:
                        pe.wait_ge(sem(f"gated{r}_{layer}"), k + 1)
                        for f in range(C):
                            if k == 0 and (r or layer):
                                pe.wait_ge(sem(f"G0_{layer}" if r else "rel0_out"), f + 1)
                            mm = pe.matmul(bank[f][:, :], g[:, k, blk(P, f)], cnt[:, r, k, :],
                                           start=(k == 0), stop=(k == C - 1))
                            if k == C - 1:
                                mm.then_inc(sem(f"G{r}_{layer}_psum"), 1)

                def rel_tile(layer, c):
                    w = weight(f"root{layer + 1}")
                    pe.wait_ge(sem(f"G1_{layer}"), c + 1)
                    for k in range(C):
                        pe.matmul(bank[c][:, :], hT[:, k, blk(P, c)], w[:, k, :], start=(k == 0), stop=False)
                    if c == 0:
                        pe.wait_ge(sem("w_loaded"), 16 * (layer + 1))
                        pe.wait_ge(sem(f"G1_{layer}"), C)
                    for r, g in ((0, vr), (1, adjT)):
                        for k in range(C):
                            mm = pe.matmul(bank[c][:, :], g[:, k, blk(P, c)], qkw[:, r * C + k, :],
                                           start=False, stop=(r == 1 and k == C - 1))
                    mm.then_inc(sem(f"rel{layer}_psum"), 1)

                def turn_rel(layer, ready, c, free):
                    if c >= 2:
                        pe.wait_ge(sem(f"sigmoid{layer}"), c - 1)
                    turn(hr, c, ready, f"relT{layer}", free)

                turn_rel(0, "h_rel0", 0, "x5")
                turn_rel(0, "h_rel0", 1, "x5")
                units(56, 4)
                gates(0, 0)
                gates(0, 1)
                units(60, 2)
                turn_rel(0, "h_rel0", 2, None)
                turn_rel(0, "h_rel0", 3, None)
                units(62, 2)
                gates(0, 2)
                gates(0, 3)
                G(0, 0, range(C))
                G(0, 1, range(C))
                need_weight(pe, "root1")
                rel_tile(0, 0)
                rel_tile(0, 1)
                for c in range(C - 1):
                    turn_rel(1, "rel0_out", c, "sigmoid0")
                    gates(1, c)
                    if c + 2 < C:
                        rel_tile(0, c + 2)
                G(1, 0, (0,))
                turn_rel(1, "rel0_out", C - 1, None)
                gates(1, C - 1)
                G(1, 0, range(1, C))
                G(1, 1, range(C))
                need_weight(pe, "root2")
                for c in range(C):
                    rel_tile(1, c)


def _chunked(w):
    return np.ascontiguousarray(w.reshape(C, P, -1).transpose(1, 0, 2))


def kernel(**inputs):
    import concourse.bacc as bacc
    from concourse.bass_utils import run_bass_kernel_spmd

    i = {k: np.asarray(v) for k, v in inputs.items()}
    edge = {k: np.ascontiguousarray(i[k].reshape(ECH, P).T) for k in ("src", "dst", "edge_type_2")}
    w1, w2 = i["L0_gnn_W1"], i["L0_gnn_W2"]
    conv1, conv2 = i["L1_gnn_conv_W1"], i["L1_gnn_conv_W2"]
    weights = np.stack([_chunked(w) for w in (
        i["L0_gnn_Wq"], i["L0_gnn_Wk"], i["L0_gnn_Wv"], i["L0_gnn_Wo"], w1[:, :D], w1[:, D:], w2[:D], w2[D:],
        i["L1_gnn_lin_W"].T, conv1[0].T, conv2[0].T, conv1[1].T, conv2[1].T,
        i["L2_gnn_W"], i["L3_gnn_root1"], i["L3_gnn_root2"])])
    rows = np.stack([i[k] for k in (
        "L0_gnn_bv", "L0_gnn_bo", "L0_gnn_g1", "L0_gnn_be1", "L0_gnn_b2", "L0_gnn_g2", "L0_gnn_be2",
        "L1_gnn_lin_b", "L1_gnn_lin_a", "L2_gnn_b", "L3_gnn_bias1", "L3_gnn_bias2")])
    cols = np.concatenate([i[k].reshape(-1, P).T for k in (
        "L0_gnn_bq", "L0_gnn_bk", "L0_gnn_b1", "L1_gnn_conv_b1", "L1_gnn_conv_b2", "L1_gnn_bn_gamma",
        "L1_gnn_bn_beta")] + [
            i[k][:, :, 0].reshape(RELS, C, P).transpose(2, 1, 0).reshape(P, -1)
            for k in ("L3_gnn_gate_w1", "L3_gnn_gate_w2")], axis=1)
    basis = np.concatenate([
        i[k].reshape(BASES, C, COLT, UNITS, D).transpose(3, 1, 0, 2, 4).reshape(UNITS, KB, COLT, D)
        for k in ("L3_gnn_basis1", "L3_gnn_basis2")])
    att = np.stack([i["L3_gnn_att1"], i["L3_gnn_att2"]])
    arrays = {"x": _chunked(i["x"]), "src": edge["src"], "dst": edge["dst"], "etype": edge["edge_type_2"],
              "weights": weights, "rows": rows, "cols": cols, "alphas": i["L1_gnn_conv_a"], "att": att,
              "basis": basis}
    arrays = {k: np.ascontiguousarray(a) for k, a in arrays.items()}

    nc = bacc.Bacc("TRN2", target_bir_lowering=False, num_devices=1)
    args = [nc.dram_tensor(f"in_{k}", a.shape, mybir.dt.from_np(a.dtype), kind="ExternalInput").ap()
            for k, a in arrays.items()]
    scratch = nc.dram_tensor("w_scratch", (2, P, Q, D), F32, kind="Internal").ap()
    out = nc.dram_tensor("out_0", (P, C, D), F32, kind="ExternalOutput").ap()
    build(nc, *args, scratch, out)
    r = run_bass_kernel_spmd(nc, [{f"in_{k}": a for k, a in arrays.items()}], core_ids=[0])
    return np.ascontiguousarray(r.results[0]["out_0"].transpose(1, 0, 2)).reshape(N, D)
```

```python
from contextlib import ExitStack

import concourse.bass as bass
import numpy as np
from concourse import mybir

F32 = mybir.dt.float32
F32R = mybir.dt.float32r
BF16 = mybir.dt.bfloat16
F16 = mybir.dt.float16
I32 = mybir.dt.int32
ALU = mybir.AluOpType
ACT = mybir.ActivationFunctionType

P = 128
N = 512
D = 512
C = D // P
HEADS = 8
HD = D // HEADS
EDGES = 16896
ECH = EDGES // P
LN_EPS = 1e-5

FIELDS = 2 * C
FBITS = 3
UNIT_BITS = FBITS * (FIELDS - 1)
TOO_MANY = 1.0e6
HOT = 16
FIRST_TILE, TILE_EVERY = 2, 10
TILE_LAG = 8


def act_hots(n):
    return n // 5 * 3 + (0, 0, 1, 1, 2)[n % 5]


def on_act(n):
    return act_hots(n + 1) > act_hots(n)


assert EDGES % P == 0 and FBITS * FIELDS <= 24

BASES = 30
RELS = 2
KB = C * BASES
Q = RELS * C
COLT = 4
UNITS = P // COLT
BATCH = 4
BATCHES = UNITS // BATCH
EARLY_UNITS = 4

WEIGHTS = ("q", "k", "v", "o", "f1a", "f1b", "f2a", "f2b", "lin",
           "c1_0", "c2_0", "c1_1", "c2_1", "gcn", "root1", "root2")
PLACE = {"q": 0, "k": 1, "v": 2, "o": 3, "f1a": "hT", "f1b": "hT", "f2a": "hT", "f2b": 0, "lin": 1,
         "c1_0": "hT", "c2_0": "hT", "c1_1": "hT", "c2_1": "hT", "gcn": "hT", "root1": 2, "root2": 3}
PARTS = {"f1a": (0, "k_psum", C), "f1b": (1, "o_psum", C), "lin": (1, "ff1_psum", 2 * C),
         "c1_0": (0, "ff2_psum", C), "c2_0": (1, "lin_psum", C), "c1_1": (0, "c1_0_psum", C),
         "c2_1": (1, "c2_0_psum", C), "gcn": (0, "c1_1_psum", C)}
IN_PARTS = tuple(PARTS)
LAST_READ = {"f1a": ("v_psum", C), "f1b": ("weight_parts", C), "f2a": ("weight_parts", 2 * C),
             "f2b": ("ff1_psum", C), "lin": ("ff1_psum", C), "c1_0": ("ff2_psum", C),
             "c2_0": ("weight_parts", 4 * C), "c1_1": ("weight_parts", 5 * C),
             "c2_1": ("weight_parts", 6 * C), "gcn": ("weight_parts", 7 * C),
             "root1": ("c2_1_psum", C), "root2": ("c2_1_psum", C)}
T_ORDER = ("h1T", "hT2", "agg0", "agg1", "agg2")

ROWS = ("bv", "bo", "g1", "be1", "b2", "g2", "be2", "lin_b", "lin_a", "gcn_b", "bias1", "bias2")
RSLOTS = 5

COLS = {}
for _name, _n in (("bq", C), ("bk", C), ("b1", 2 * C), ("c1b", 2 * C), ("c2b", 2 * C), ("gam", 2 * C),
                  ("bet", 2 * C), ("gw1", RELS * C), ("gw2", RELS * C)):
    COLS[_name] = sum(n for _, n in COLS.values()), _n
NCOLS = sum(n for _, n in COLS.values())


def build(nc, x, src, dst, etype, weights, rows, cols, alphas, att, basis, scratch, out):
    with ExitStack() as ctx:
        def sb(name, shape, dt=F32):
            return ctx.enter_context(nc.sbuf_tensor(name, shape, dt))

        names = {}

        def sem(name):
            if name not in names:
                names[name] = ctx.enter_context(nc.semaphore(name))
            return names[name]

        bank = [ctx.enter_context(nc.psum_tensor(f"bank{i}", [P, N], F32)) for i in range(8)]

        def places(first, then):
            with ExitStack() as early:
                a = [early.enter_context(nc.sbuf_tensor(*t)) for t in first]
            return a + [ctx.enter_context(nc.sbuf_tensor(*t)) for t in then]

        xr = sb("xr", [P, C, D])
        hr = sb("hr", [P, C, D])
        hT = sb("hT", [P, C, D])
        qkw, hT_hi, hT_lo = places(
            [("qkw", [P, 2 * C, D], F32)], [("hT_hi", [P, C, D], F32R), ("hT_lo", [P, C, D], F32R)])
        no_edge, adjT_r = places([("no_edge", [P, C, N], F32)], [("adjT_r", [P, C, N], F32R)])
        qT, kT = qkw[:, 0:C, :], qkw[:, C:2 * C, :]
        cnt = sb("cnt", [P, 2, C, N])
        vr, adjT, G0_hi, G0_lo = places(
            [("vr", [P, C, D], F32), ("adjT", [P, C, N], F32)],
            [("G0_hi", [P, C, D], F32R), ("G0_lo", [P, C, D], F32R)])
        s01, gated0_hi, gated0_lo = places(
            [("s01", [P, 2 * C, D], F32)],
            [("gated0_hi", [P, C, D], F32R), ("gated0_lo", [P, C, D], F32R)])
        s0, s1 = s01[:, 0:C, :], s01[:, C:2 * C, :]
        bring, w_hi, w_lo = places(
            [("bring", [P, BATCH, COLT, D], F32)],
            [("w_hi", [P, 2 * C, D], F32R), ("w_lo", [P, 2 * C, D], F32R)])
        stage, G1_hi, G1_lo = places(
            [("stage", [P, 2, BATCH, D], F32)],
            [("G1_hi", [P, C, D], F32R), ("G1_lo", [P, C, D], F32R)])
        wring01, w0_hi, w0_lo = places(
            [("wring01", [P, 2, C, D], F32)], [("w0_hi", [P, C, D], F32R), ("w0_lo", [P, C, D], F32R)])
        wring23, w1_hi, w1_lo = places(
            [("wring23", [P, 2, C, D], F32)], [("w1_hi", [P, C, D], F32R), ("w1_lo", [P, C, D], F32R)])
        cnt_r = (w0_hi, w0_lo)
        softmax_tmp, edge_i, dst_part, edge_f, edge_w, _, gated1_hi, gated1_lo = places(
            [("softmax_tmp", [P, C, N // 2], F32), ("edge_i", [P, 3, ECH], I32),
             ("dst_part", [P, 2, ECH], I32), ("edge_f", [P, 5, ECH], F32), ("edge_w", [P, ECH], I32),
             ("unused", [P, 2 * C * D - C * N // 2 - 11 * ECH], F32)],
            [("gated1_hi", [P, C, D], F32R), ("gated1_lo", [P, C, D], F32R)])
        x_hi, x_lo = gated1_hi, gated1_lo
        src_f, dst_lo, rel1, field, minus_w = (edge_f[:, a, :] for a in range(5))
        weight_f = edge_w[:, :].bitcast(F32)
        rring = sb("rring", [P, RSLOTS, D])
        colsb = sb("colsb", [P, NCOLS])
        alph = sb("alph", [P, 2])
        attw = sb("attw", [P, 2, 32])
        ident = sb("ident", [P, P])
        bq8 = sb("bq8", [P, C])
        stat = sb("stat", [P, 8, C, 12])
        gcn_s = sb("gcn_s", [P, C, 8])
        gate = sb("gate", [P, 2, C, RELS])
        iota = sb("iota_row", [P, N], F16)
        ones = sb("ones", [P, 1])
        distance = sb("distance", [P, 2, P], BF16)
        zeros = sb("zeros", [P, N], BF16)
        tally = sb("tally", [P, 4])
        flag = sb("flag", [1, 1], I32)
        hot_s = cnt[:, :, :, :].rearrange("p r c n -> p (r c n)").bitcast(BF16).rearrange("p (r n) -> p r n", r=HOT)
        hot_d = adjT[:, 0:2, :].rearrange("p a n -> p (a n)").bitcast(BF16).rearrange("p (r n) -> p r n", r=HOT)
        packed = adjT[:, 3, :].bitcast(I32)
        digits = s01[:, :, :].bitcast(I32)

        def col(name, i=0, n=1):
            at = COLS[name][0]
            return colsb[:, at + i:at + i + n]

        def row(name):
            return rring[:, ROWS.index(name) % RSLOTS, :]

        def weight(name):
            slot = PLACE[name]
            return hT[:, :, :] if slot == "hT" else (wring01, wring23)[slot // 2][:, slot % 2, :, :]

        def weight_parts(name):
            return ((w0_hi, w0_lo), (w1_hi, w1_lo))[PARTS[name][0]]

        def need_row(eng, name):
            i = ROWS.index(name)
            eng.wait_ge(sem(f"row_slot{i % RSLOTS}_loaded"), 16 * (i // RSLOTS + 1))

        def need_weight(eng, name):
            place = [w for w in WEIGHTS if PLACE[w] == PLACE[name]]
            eng.wait_ge(sem(f"weight_{PLACE[name]}_loaded"), 16 * (place.index(name) + 1))

        def st(use, c, a, b=None):
            return stat[:, use, c, a:(a + 1 if b is None else b)]

        def norms(use, c):
            return 2 * C + 2 * c + use - 1 if use in (2, 3) else use * C + c + 1

        def blk(t, c):
            return slice(c * t, (c + 1) * t)

        with nc.Block() as block:

            @block.sync
            def _(sp):
                for i, e in enumerate((src, dst, etype)):
                    sp.dma_start(edge_i[:, i, :], e).then_inc(sem("edges_loaded"), 16)
                sp.dma_start(xr[:, :, :], x).then_inc(sem("x_loaded"), 16)
                sp.dma_start(colsb[:, :], cols).then_inc(sem("cols_loaded"), 16)
                sp.dma_start(alph[:, :], alphas.partition_broadcast(P)).then_inc(sem("cols_loaded"), 16)
                sp.wait_ge(sem("att_zero"), 1)
                for layer in range(2):
                    for c in range(C):
                        for r in range(RELS):
                            q = r * C + c
                            sp.dma_start(attw[c * BASES:(c + 1) * BASES, layer, q:q + 1],
                                         att[layer, r, :].rearrange("(b a) -> b a", a=1)).then_inc(
                                             sem("att_loaded"), 16)
                for n in range(2 * UNITS + BATCH):
                    if n < 2 * UNITS:
                        if n >= BATCH:
                            sp.wait_ge(sem("basis_used"), n - BATCH + 1)
                        sp.dma_start(bring[0:KB, n % BATCH, :, :], basis[n]).then_inc(
                            sem(f"basis{n % BATCH}_loaded"), 16)
                    if n % BATCH == BATCH - 1 and n >= 2 * BATCH - 1:
                        b = n // BATCH - 1
                        sp.wait_ge(sem("stage_ready"), (b + 1) * BATCH)
                        layer, g = divmod(b, BATCHES)
                        for j in range(COLT):
                            at = j * UNITS + g * BATCH
                            sp.dma_start(scratch[layer, at:at + BATCH, :, :].rearrange("g q o -> q g o"),
                                         stage[32 * j:32 * j + Q, b % 2, :, :]).then_inc(sem(f"w_stored{b % 2}"), 16)
                for c in range(C):
                    sp.wait_ge(sem("rel1_out_sum"), c + 1)
                    sp.dma_start(out[:, c, :], hr[:, c, :]).then_inc(sem("out_stored"), 16)
                sp.wait_ge(sem("out_stored"), 16 * C)

            @block.gpsimd
            def _(pool):
                pool.memset(attw[:, :, :], 0.0).then_inc(sem("att_zero"), 1)
                pool.iota(iota[:, :], [[1, N]], base=0, channel_multiplier=0,
                          allow_small_or_imprecise_dtypes=True).then_inc(sem("iota"), 1)
                pool.memset(zeros[:, :], 0.0).then_inc(sem("zeros"), 1)
                pool.memset(ones[:, :], 1.0).then_inc(sem("ones"), 1)
                pool.memset(ident[:, :], 0.0).then_inc(sem("ident0"), 1)
                pool.wait_ge(sem("ident0"), 1)
                pool.affine_select(out=ident[:, :], in_=ident[:, :], compare_op=ALU.not_equal, fill=1.0,
                                   base=0, pattern=[[-1, P]], channel_multiplier=1).then_inc(sem("ident"), 1)

                for i in range(4):
                    pool.dma_start(weight(WEIGHTS[i]), weights[i]).then_inc(sem(f"weight_{i}_loaded"), 16)
                for i in range(RSLOTS):
                    pool.dma_start(row(ROWS[i]), rows[i, :].partition_broadcast(P)).then_inc(
                        sem(f"row_slot{i}_loaded"), 16)

                def load_weight(name):
                    i = WEIGHTS.index(name)
                    last, tiles = LAST_READ[name]
                    pool.wait_ge(sem(last), tiles)
                    pool.dma_start(weight(name), weights[i]).then_inc(sem(f"weight_{PLACE[name]}_loaded"), 16)

                def load_row(name, last):
                    i = ROWS.index(name)
                    pool.wait_ge(sem(last), C)
                    pool.dma_start(row(name), rows[i, :].partition_broadcast(P)).then_inc(
                        sem(f"row_slot{i % RSLOTS}_loaded"), 16)

                def load_w(layer):
                    for par in range(2):
                        pool.wait_ge(sem(f"w_stored{par}"), (layer + 1) * (BATCHES // 2) * COLT * 16)
                    if layer:
                        pool.wait_ge(sem("w_lo"), RELS)
                    else:
                        pool.wait_ge(sem("gcn_psum"), C)
                    pool.dma_start(qkw[:, :, :], scratch[layer]).then_inc(sem("w_loaded"), 16)

                load_row("g2", "v")
                load_weight("f1a")
                load_row("be2", "h_plus_bo")
                load_weight("f1b")
                load_row("lin_b", "h1")
                load_row("lin_a", "h1")
                load_weight("f2a")
                load_row("gcn_b", "h1_plus_b2")
                for n in ("f2b", "lin", "c1_0"):
                    load_weight(n)
                load_row("bias1", "x1")
                load_row("bias2", "x_plus")
                for n in ("c2_0", "c1_1", "c2_1", "gcn", "root1", "root2"):
                    load_weight(n)
                load_w(0)
                load_w(1)

            @block.scalar
            def _(act):
                def root(use, c):
                    act.wait_ge(sem("var_inverse"), norms(use, c))
                    act.activation(st(use, c, 9), st(use, c, 8), ACT.Sqrt).then_inc(sem("rstd"), 1)

                def relu_norm(use, c, done):
                    root(use, c)
                    act.wait_ge(sem(f"nbias{use}"), c + 1)
                    act.activation(hr[:, c, :], xr[:, c, :], ACT.Relu, scale=st(use, c, 9),
                                   bias=st(use, c, 10)).then_inc(sem(done), 1)

                def turn(done, dest, c):
                    act.wait_ge(sem(done + "_psum"), c + 1)
                    act.copy(dest[:, :, blk(P, c)],
                             bank[4 + c % 2][:, :].rearrange("p (f n) -> p f n", f=C)).then_inc(
                                 sem("T_hi" if done in T_ORDER else done), 1)

                def split_weight(name):
                    need_weight(act, name)
                    act.wait_ge(sem(PARTS[name][1]), PARTS[name][2])
                    if name == "c1_0":
                        act.wait_ge(sem("weight_parts"), 3 * C)
                    for k in range(C):
                        act.copy(weight_parts(name)[0][:, k, :], weight(name)[:, k, :]).then_inc(
                            sem("weight_hi"), 1)

                def take(done, dest, c, bias=0.0, func=ACT.Identity, b=None):
                    act.wait_ge(sem(done + "_psum"), c + 1)
                    act.activation(dest, bank[c % C][:, :], func, bias=bias).then_inc(
                        sem("T_hi" if done in T_ORDER else b or done), 1)

                unit = iter(range(2 * UNITS))

                def stage_units(n):
                    for u in (next(unit) for _ in range(n)):
                        b = u // BATCH
                        act.wait_ge(sem("basis_used"), u + 1)
                        if b >= 2 and u % BATCH == 0:
                            act.wait_ge(sem(f"w_stored{b % 2}"), (b // 2) * COLT * 16)
                        act.copy(stage[:, b % 2, u % BATCH, :], bank[6 + u % 2][:, :]).then_inc(
                            sem("stage_ready"), 1)

                def qk_take(t):
                    which, c = divmod(t, C)
                    if which == 0:
                        act.wait_ge(sem("bq8"), 1)
                        act.wait_ge(sem("q_psum"), c + 1)
                        act.activation(qT[:, c, :], bank[c][:, :], ACT.Identity, scale=HD ** -0.5,
                                       bias=bq8[:, c:c + 1]).then_inc(sem("q"), 1)
                    else:
                        take("k", kT[:, c, :], c, col("bk", c))

                def distances(i):
                    n = my_chunks[i]
                    if i >= 2:
                        act.wait_ge(sem("act_hot_ready"), i - 1)
                    act.activation(distance[:, i % 2, :], iota[:, 0:P], ACT.Abs, scale=-1.0,
                                   bias=dst_lo[:, n:n + 1]).then_inc(sem("distance"), 1)

                my_chunks = [n for n in range(ECH) if on_act(n)]
                for c in range(C):
                    root(0, c)
                for c in range(C):
                    act.wait_ge(sem("nbias0"), c + 1)
                    act.activation(hr[:, c, :], xr[:, c, :], ACT.Relu, scale=st(0, c, 9),
                                   bias=st(0, c, 10)).then_inc(sem("h0"), 1)
                act.wait_ge(sem("edge_step"), 8)
                act.wait_ge(sem("iota"), 1)
                distances(0)
                for c in range(C):
                    turn("hT0", hT, c)
                for n in range(ECH):
                    if on_act(n):
                        i = act_hots(n)
                        if i + 1 < len(my_chunks):
                            distances(i + 1)
                        act.wait_ge(sem("distance"), i + 1)
                        if n >= HOT:
                            act.wait_ge(sem("hot_used"), n - HOT + 1)
                        act.activation(hot_d[:, n % HOT, :], distance[:, i % 2, :], ACT.Relu,
                                       scale=minus_w[:, n:n + 1], bias=weight_f[:, n:n + 1]).then_inc(
                                           sem("act_hot_ready"), 1)
                    t, at = divmod(n - FIRST_TILE - TILE_LAG, TILE_EVERY)
                    if at == 0 and 0 <= t < 2 * C:
                        if t == 0:
                            act.wait_ge(sem("cols_loaded"), 32)
                        qk_take(t)
                stage_units(EARLY_UNITS)
                act.wait_ge(sem("digits"), C)
                act.activation(cnt[:, 0, :, :], digits[:, 0:C, :], ACT.Copy,
                               accum_out=tally[:, 0:1]).then_inc(sem("counts0"), 1)
                def take_scores(it):
                    if it >= 2:
                        act.wait_ge(sem("pv_used"), it - 1)
                    for q in range(4):
                        h0 = 4 * (q // 2) + q % 2
                        heads = s01[:, (it % 2) * C:(it % 2 + 1) * C, :].rearrange("p c (a n) -> p (c a) n", a=2)
                        act.wait_ge(sem("scores_psum"), it * 4 + q + 1)
                        act.copy(heads[:, h0:h0 + 3:2, :],
                                 bank[4 + q % 2][:, :].rearrange("p (a n) -> p a n", a=2)).then_inc(
                                     sem("scores"), 1)

                act.wait_ge(sem("no_edge"), 1)
                take_scores(0)
                for it in range(2 * C):
                    for half in range(2):
                        act.wait_ge(sem("centred"), 2 * it + half + 1)
                        sc = s01[:, (it % 2) * C + 2 * half:(it % 2) * C + 2 * half + 2, :]
                        act.activation(sc, sc, ACT.Exp).then_inc(sem("exped"), 1)
                    if it + 1 < 2 * C:
                        take_scores(it + 1)
                    stage_units(BATCH)
                    if it == 0:
                        split_weight("f1a")
                act.wait_ge(sem("pv_used"), 2 * C)
                for c in range(C):
                    act.copy(s0[:, c, :], bank[c][:, :]).then_inc(sem("ao"), 1)
                stage_units(2)
                root(1, 0)
                root(1, 1)
                turn("adjT", adjT, 0)
                turn("adjT", adjT, 1)
                root(1, 2)
                turn("adjT", adjT, 2)
                turn("adjT", adjT, 3)
                root(1, 3)
                stage_units(4)
                for c in range(C):
                    turn("h1T", hT_hi, c)
                split_weight("f1b")
                for t in range(2 * C):
                    take("ff1", s01[:, t, :], t, col("b1", t), ACT.Relu)
                stage_units(2)
                split_weight("lin")
                for c in range(C):
                    if c == C - 1:
                        turn("hT2", hT_hi, 0)
                        turn("hT2", hT_hi, 1)
                    root(2, c)
                    if c == C - 1:
                        turn("hT2", hT_hi, 2)
                    relu_norm(3, c, "h2")
                turn("hT2", hT_hi, 3)
                split_weight("c1_0")
                def batch_norm(l, c):
                    act.wait_ge(sem(f"bnb{l}"), c + 1)
                    act.activation(s1[:, c, :], s1[:, c, :], ACT.Relu, scale=st(4 + l, c, 10),
                                   bias=st(4 + l, c, 11)).then_inc(sem(f"bn{l}"), 1)

                def x3_hi(c):
                    act.wait_ge(sem("x3_psum"), c + 1)
                    act.copy(x_hi[:, :, blk(P, c)],
                             bank[4 + c % 2][:, :].rearrange("p (f n) -> p f n", f=C)).then_inc(sem("x3_hi"), 1)

                for c in range(C):
                    if c == 0:
                        stage_units(2)
                    act.wait_ge(sem("agg0_psum"), c + 1)
                    act.copy(hT_hi[:, c, :], bank[C + c][:, :]).then_inc(sem("T_hi"), 1)
                split_weight("c2_0")
                for l in range(2):
                    for c in range(C):
                        take(f"c1_{l}", s0[:, c, :], c, col("c1b", l * C + c), b=f"c1_{l}_sum")
                    if l == 0:
                        stage_units(2)
                    split_weight("gcn" if l else "c1_1")
                    take(f"c2_{l}", s1[:, 0, :], 0, col("c2b", l * C))
                    take(f"c2_{l}", s1[:, 1, :], 1, col("c2b", l * C + 1))
                    root(4 + l, 0)
                    root(4 + l, 1)
                    take(f"c2_{l}", s1[:, 2, :], 2, col("c2b", l * C + 2))
                    batch_norm(l, 0)
                    root(4 + l, 2)
                    batch_norm(l, 1)
                    take(f"c2_{l}", s1[:, 3, :], 3, col("c2b", l * C + 3))
                    if l == 0:
                        batch_norm(0, 2)
                        root(4, 3)
                        x3_hi(0)
                        x3_hi(1)
                        batch_norm(0, 3)
                        stage_units(2)
                        take("agg1", hT_hi[:, 0, :], 0)
                        x3_hi(2)
                        take("agg1", hT_hi[:, 1, :], 1)
                        x3_hi(3)
                        take("agg1", hT_hi[:, 2, :], 2)
                        take("agg1", hT_hi[:, 3, :], 3)
                        split_weight("c2_1")
                        stage_units(2)
                    else:
                        batch_norm(1, 2)
                        root(5, 3)
                        stage_units(1)
                        batch_norm(1, 3)
                        stage_units(1)
                act.wait_ge(sem("deg"), 1)
                act.activation(gcn_s[:, :, 2], gcn_s[:, :, 1], ACT.Sqrt).then_inc(sem("dinv"), 1)
                root(6, 0)
                for c in range(C):
                    if c + 1 < C:
                        root(6, c + 1)
                    act.wait_ge(sem("gcn_nb"), c + 1)
                    act.activation(hr[:, c, :], xr[:, c, :], ACT.Relu, scale=gcn_s[:, c, 3:4],
                                   bias=gcn_s[:, c, 4:5]).then_inc(sem("h_gcn"), 1)
                    act.wait_ge(sem("h_gcn"), c + 1)
                    act.copy(x_hi[:, c, :], hr[:, c, :]).then_inc(sem("h_gcn_hi"), 1)
                    if c < 2:
                        stage_units(2)
                for c in range(C):
                    take("agg2", hT_hi[:, c, :], c)
                stage_units(2)
                def gates(layer, c):
                    act.wait_ge(sem("gates_psum"), layer * C + c + 1)
                    act.activation(gate[:, layer, c, :], bank[4 + c % 2][:, 0:RELS], ACT.Sigmoid).then_inc(
                        sem("sigmoid"), 1)

                def gated(layer, c):
                    act.wait_ge(sem("sigmoid"), layer * C + c + 1)
                    for rel, g in enumerate((gated0_hi, gated1_hi)):
                        act.activation(g[:, c, :], hr[:, c, :], ACT.Copy,
                                       scale=gate[:, layer, c, rel:rel + 1]).then_inc(sem("gated_hi"), 1)

                def G_hi(layer, rel):
                    for c in range(C):
                        act.wait_ge(sem(f"G{rel}_psum"), layer * C + c + 1)
                        act.copy((G0_hi, G1_hi)[rel][:, c, :], bank[rel * C + c][:, :]).then_inc(sem("G_hi"), 1)

                def split_w(layer, rel):
                    if layer:
                        act.wait_ge(sem("rel_psum"), C)
                    else:
                        act.wait_ge(sem("basis_used"), 2 * UNITS)
                    act.wait_ge(sem("w_loaded"), 16 * (layer + 1))
                    act.copy(w_hi[:, blk(C, rel), :], qkw[:, blk(C, rel), :]).then_inc(sem("w_hi"), 1)

                act.wait_ge(sem("weight_parts"), len(IN_PARTS) * C)

                def relu7(c):
                    act.wait_ge(sem("nbias7"), c + 1)
                    act.activation(hr[:, c, :], xr[:, c, :], ACT.Relu, scale=st(7, c, 9),
                                   bias=st(7, c, 10)).then_inc(sem("h_rel0"), 1)

                root(7, 0)
                root(7, 1)
                relu7(0)
                turn("relT0", hT, 0)
                root(7, 2)
                relu7(1)
                stage_units(2)
                turn("relT0", hT, 1)
                root(7, 3)
                relu7(2)
                relu7(3)
                gates(0, 0)
                gates(0, 1)
                stage_units(2)
                turn("relT0", hT, 2)
                turn("relT0", hT, 3)
                gates(0, 2)
                gates(0, 3)
                for c in range(C):
                    gated(0, c)
                split_w(0, 0)
                G_hi(0, 0)
                split_w(0, 1)
                act.wait_ge(sem("w_stored0"), (BATCHES // 2) * 2 * COLT * 16)
                act.wait_ge(sem("w_stored1"), (BATCHES // 2) * 2 * COLT * 16)
                G_hi(0, 1)
                for c in range(C):
                    turn("relT1", hT, c)
                    gates(1, c)
                    gated(1, c)
                split_w(1, 0)
                G_hi(1, 0)
                split_w(1, 1)
                G_hi(1, 1)

            @block.vector
            def _(dve):
                steps = [0]

                def step(ins):
                    steps[0] += 1
                    ins.then_inc(sem("dve_step"), 1)
                    return steps[0]

                def after(n):
                    dve.wait_ge(sem("dve_step"), n)

                dve.wait_ge(sem("edges_loaded"), 48)
                dve.tensor_copy(src_f, edge_i[:, 0, :]).then_inc(sem("edge_step"), 1)
                dve.tensor_scalar(dst_part[:, 0, :], edge_i[:, 1, :], P - 1, None, ALU.bitwise_and).then_inc(
                    sem("edge_step"), 1)
                dve.tensor_scalar(dst_part[:, 1, :], edge_i[:, 1, :], P.bit_length() - 1, None,
                                  ALU.logical_shift_right).then_inc(sem("edge_step"), 1)
                dve.tensor_scalar(rel1, edge_i[:, 2, :], 0.0, None, ALU.not_equal).then_inc(sem("edge_step"), 1)
                dve.wait_ge(sem("edge_step"), 4)
                dve.tensor_copy(dst_lo, dst_part[:, 0, :]).then_inc(sem("edge_step"), 1)
                dve.scalar_tensor_tensor(field, rel1, float(C), dst_part[:, 1, :], ALU.mult, ALU.add).then_inc(
                    sem("edge_step"), 1)
                dve.wait_ge(sem("edge_step"), 6)
                dve.tensor_scalar(edge_w[:, :], field, -FBITS * 2.0 ** 23, 127 * 2.0 ** 23, ALU.mult,
                                  ALU.add).then_inc(sem("edge_step"), 1)
                dve.wait_ge(sem("edge_step"), 7)
                dve.tensor_scalar(minus_w[:, :], weight_f, -1.0, None, ALU.mult).then_inc(sem("edge_step"), 1)
                dve.wait_ge(sem("iota"), 1)

                def one_hots(n):
                    if n >= HOT:
                        dve.wait_ge(sem("hot_used"), n - HOT + 1)
                    if not on_act(n):
                        dve.tensor_scalar(hot_d[:, n % HOT, :], iota[:, 0:P], dst_lo[:, n:n + 1],
                                          weight_f[:, n:n + 1], ALU.is_equal, ALU.mult).then_inc(
                                              sem("hot_ready"), 1)
                    dve.tensor_scalar(hot_s[:, n % HOT, :], iota[:, :], src_f[:, n:n + 1], None,
                                      ALU.is_equal).then_inc(sem("hot_ready"), 1)

                def norm_stats(use, t, c):
                    after(step(dve.bn_stats(st(use, c, 0, 6), t)))
                    after(step(dve.bn_aggr(st(use, c, 6, 8), st(use, c, 0, 6))))
                    after(step(dve.tensor_scalar(st(use, c, 7), st(use, c, 7), LN_EPS, None, ALU.add)))
                    dve.reciprocal(st(use, c, 8), st(use, c, 7)).then_inc(sem("var_inverse"), 1)

                def nbias(use, c):
                    dve.wait_ge(sem("rstd"), norms(use, c))
                    dve.tensor_scalar(st(use, c, 10), st(use, c, 6), st(use, c, 9), -1.0, ALU.mult,
                                      ALU.mult).then_inc(sem(f"nbias{use}"), 1)

                def take_v(c):
                    if c == 0:
                        need_row(dve, "bv")
                    dve.wait_ge(sem("v_psum"), c + 1)
                    dve.tensor_tensor(vr[:, c, :], bank[c][:, :], row("bv"), ALU.add).then_inc(sem("v"), 1)

                dve.wait_ge(sem("x_loaded"), 16)
                for c in range(C):
                    norm_stats(0, xr[:, c, :], c)
                for c in range(C):
                    nbias(0, c)
                dve.wait_ge(sem("cols_loaded"), 32)
                dve.tensor_scalar(bq8[:, :], col("bq", 0, C), HD ** -0.5, None, ALU.mult).then_inc(sem("bq8"), 1)
                for n in range(ECH):
                    one_hots(n)
                    t, at = divmod(n - FIRST_TILE - TILE_LAG, TILE_EVERY)
                    if at == 0 and 2 * C <= t < 3 * C:
                        take_v(t - 2 * C)
                for t in range(max(2 * C, (ECH - 1 - FIRST_TILE - TILE_LAG) // TILE_EVERY + 1), 3 * C):
                    take_v(t - 2 * C)
                dve.wait_ge(sem("hot_used"), ECH)
                dve.tensor_scalar(packed, bank[7][:, :], 2.0 ** UNIT_BITS, None, ALU.mult).then_inc(
                    sem("packed"), 1)
                dve.reduce_max(tally[:, 2:3], bank[7][:, :], axis=mybir.AxisListType.X).then_inc(sem("packed"), 1)
                dve.wait_ge(sem("packed"), 2)
                for f in range(FIELDS):
                    dve.tensor_scalar(digits[:, f, :], packed, FBITS * (FIELDS - 1 - f), 2 ** FBITS - 1,
                                      ALU.logical_shift_right, ALU.bitwise_and).then_inc(sem("digits"), 1)
                dve.wait_ge(sem("digits"), FIELDS)
                dve.tensor_scalar(cnt[:, 1, :, :], digits[:, C:2 * C, :], 0.0, 0.0, ALU.add, ALU.add,
                                  accum_out=tally[:, 1:2]).then_inc(sem("counts1"), 1)
                dve.tensor_scalar(tally[:, 3:4], tally[:, 2:3], 2.0 ** FBITS, TOO_MANY, ALU.is_ge,
                                  ALU.mult).then_inc(sem("tally_step"), 1)
                dve.wait_ge(sem("counts0"), 1)
                dve.wait_ge(sem("counts1"), 1)
                dve.wait_ge(sem("tally_step"), 1)
                dve.scalar_tensor_tensor(tally[:, 3:4], tally[:, 3:4], tally[:, 0:1], tally[:, 1:2], ALU.add,
                                         ALU.add).then_inc(sem("tally"), 1)
                dve.wait_ge(sem("tally_sum"), 1)
                dve.tensor_scalar(flag[:, :], bank[6][0:1, 0:1], float(EDGES), None, ALU.is_equal).then_inc(
                    sem("flag"), 1)
                dve.wait_ge(sem("flag"), 1)
                fits = dve.value_load(flag[0:1, 0:1])
                with dve.If(fits < 1):
                    slow_d = s0[:, 0, 0:N // 2].bitcast(BF16)
                    slow_s = s0[:, 1, 0:N // 2].bitcast(BF16)
                    dst_f, rel_f = field, dst_lo
                    dve.tensor_copy(dst_f, edge_i[:, 1, :]).then_inc(sem("slow_step"), 1)
                    for r in range(RELS):
                        dve.tensor_scalar(rel_f, rel1, float(r), None, ALU.is_equal).then_inc(sem("slow_step"), 1)
                        dve.wait_ge(sem("slow_step"), r + 2)
                        with dve.Fori(0, ECH) as n:
                            dve.wait_ge(sem("slow_used"), n + (r * (ECH + 1) + 1))
                            dve.tensor_scalar(slow_d, iota[:, :], dst_f[:, bass.ds(n, 1)], None,
                                              ALU.is_equal).then_inc(sem("slow_hot"), 1)
                            dve.tensor_scalar(slow_s, iota[:, :], src_f[:, bass.ds(n, 1)],
                                              rel_f[:, bass.ds(n, 1)], ALU.is_equal, ALU.mult).then_inc(
                                                  sem("slow_hot"), 1)
                        dve.wait_ge(sem("slow_counted"), r + 1)
                        for c in range(C):
                            dve.tensor_copy(cnt[:, r, c, :], bank[c][:, :]).then_inc(sem("slow_copied"), 1)
                    dve.wait_ge(sem("slow_copied"), RELS * C)

                def find_no_edge(c):
                    after(step(dve.tensor_tensor(no_edge[:, c, :], cnt[:, 0, c, :], cnt[:, 1, c, :], ALU.add)))
                    dve.tensor_scalar(no_edge[:, c, :], no_edge[:, c, :], 0.0, 1.0 / HEADS, ALU.is_equal,
                                      ALU.mult).then_inc(sem("no_edge"), 1)

                find_no_edge(0)
                NH = N // 2
                tmp = softmax_tmp

                def scores_of(it):
                    return s01[:, (it % 2) * C:(it % 2 + 1) * C, :].rearrange("p c (a n) -> p (c a) n", a=2)

                def split_weight(name, ks=range(C)):
                    hi, lo = weight_parts(name)
                    i = IN_PARTS.index(name)
                    for k in ks:
                        dve.wait_ge(sem("weight_hi"), i * C + k + 1)
                        dve.tensor_tensor(lo[:, k, :], weight(name)[:, k, :], hi[:, k, :].bitcast(F32),
                                          ALU.subtract).then_inc(sem("weight_parts"), 1)

                def T_lo(done, c):
                    dve.wait_ge(sem("T_hi"), T_ORDER.index(done) * C + c + 1)
                    if done in ("h1T", "hT2"):
                        dve.tensor_tensor(hT_lo[:, :, blk(P, c)],
                                          bank[4 + c % 2][:, :].rearrange("p (f n) -> p f n", f=C),
                                          hT_hi[:, :, blk(P, c)].bitcast(F32), ALU.subtract).then_inc(sem(done), 1)
                    else:
                        at = C + c if done == "agg0" else c
                        dve.tensor_tensor(hT_lo[:, c, :], bank[at][:, :], hT_hi[:, c, :].bitcast(F32),
                                          ALU.subtract).then_inc(sem(done), 1)

                need_row(dve, "bo")
                for it in range(2 * C):
                    sc = scores_of(it)
                    dve.wait_ge(sem("scores"), 4 * it + 4)
                    if it:
                        dve.wait_ge(sem("probs"), it)
                    after(step(dve.tensor_tensor(tmp[:, 0:4, :], sc[:, 0:4, :], sc[:, 4:8, :], ALU.max)))
                    after(step(dve.tensor_tensor(tmp[:, 0:2, :], tmp[:, 0:2, :], tmp[:, 2:4, :], ALU.max)))
                    after(step(dve.tensor_tensor(tmp[:, 0, :], tmp[:, 0, :], tmp[:, 1, :], ALU.max)))
                    for half in range(2):
                        heads = sc[:, 4 * half:4 * half + 4, :]
                        dve.tensor_tensor(heads, heads, tmp[:, 0:1, :].to_broadcast([P, 4, NH]),
                                          ALU.subtract).then_inc(sem("centred"), 1)
                    if it == 0:
                        for c in range(1, C):
                            find_no_edge(c)
                    dve.wait_ge(sem("centred"), 2 * it + 2)
                    dve.wait_ge(sem("exped"), 2 * it + 1)
                    step(dve.tensor_tensor(tmp[:, 0:2, :], sc[:, 0:2, :], sc[:, 2:4, :], ALU.add))
                    dve.wait_ge(sem("exped"), 2 * it + 2)
                    after(step(dve.tensor_tensor(tmp[:, 2:4, :], sc[:, 4:6, :], sc[:, 6:8, :], ALU.add)))
                    after(step(dve.tensor_tensor(tmp[:, 0:2, :], tmp[:, 0:2, :], tmp[:, 2:4, :], ALU.add)))
                    after(step(dve.tensor_tensor(tmp[:, 0, :], tmp[:, 0, :], tmp[:, 1, :], ALU.add)))
                    after(step(dve.reciprocal(tmp[:, 1, :], tmp[:, 0, :])))
                    half_n, m = divmod(it, C)
                    if it == 0:
                        dve.wait_ge(sem("no_edge"), C)
                    after(step(dve.scalar_tensor_tensor(tmp[:, 2, :], no_edge[:, m, blk(NH, half_n)], 0.0,
                                                        tmp[:, 1, :], ALU.is_equal, ALU.mult)))
                    dve.tensor_tensor(sc, sc, tmp[:, 2:3, :].to_broadcast([P, HEADS, NH]),
                                      ALU.mult).then_inc(sem("probs"), 1)

                def affine_norm(use, t, c, g, be, dest, done):
                    dve.wait_ge(sem("var_inverse"), norms(use, c))
                    after(step(dve.scalar_tensor_tensor(t, t, st(use, c, 6), row(g), ALU.subtract, ALU.mult)))
                    dve.wait_ge(sem("rstd"), norms(use, c))
                    dve.scalar_tensor_tensor(dest, t, st(use, c, 9), be, ALU.mult, ALU.add).then_inc(sem(done), 1)

                split_weight("f1a")
                for c in range(C):
                    dve.wait_ge(sem("hT0_psum"), c + 1)
                    dve.tensor_tensor(hr[:, c, :], hr[:, c, :], row("bo"), ALU.add).then_inc(sem("h_plus_bo"), 1)
                dve.wait_ge(sem("ident"), 1)
                for c in range(C):
                    after(step(dve.tensor_tensor(qT[:, c, :], cnt[:, 0, c, :], cnt[:, 1, c, :], ALU.add)))
                    dve.tensor_tensor(qT[:, c, blk(P, c)], qT[:, c, blk(P, c)], ident[:, :],
                                      ALU.add).then_inc(sem("adj"), 1)
                for c in range(C):
                    dve.wait_ge(sem("adj"), c + 1)
                    n = step(dve.reduce_sum(gcn_s[:, c, 0:1], qT[:, c, :], axis=mybir.AxisListType.X))
                after(n)
                dve.reciprocal(gcn_s[:, :, 1], gcn_s[:, :, 0]).then_inc(sem("deg"), 1)
                for n in ("g1", "be1", "b2", "g2"):
                    need_row(dve, n)
                for c in range(C):
                    dve.wait_ge(sem("o_psum"), c + 1)
                    dve.wait_ge(sem("h_plus_bo"), c + 1)
                    after(step(dve.tensor_tensor(vr[:, c, :], bank[c][:, :], hr[:, c, :], ALU.add)))
                    norm_stats(1, vr[:, c, :], c)
                    affine_norm(1, vr[:, c, :], c, "g1", row("be1"), vr[:, c, :], "h1")
                for c in range(C):
                    T_lo("h1T", c)
                split_weight("f1b")
                for c in range(C):
                    dve.wait_ge(sem("h1T_psum"), c + 1)
                    dve.tensor_tensor(vr[:, c, :], vr[:, c, :], row("b2"), ALU.add).then_inc(sem("h1_plus_b2"), 1)
                need_row(dve, "be2")
                for c in range(C):
                    dve.wait_ge(sem("h0"), c + 1)
                    dve.tensor_tensor(xr[:, c, :], xr[:, c, :], row("be2"), ALU.add).then_inc(sem("x_plus"), 1)
                dve.wait_ge(sem("adjT"), C)
                for c in range(C):
                    dve.tensor_copy(adjT_r[:, c, :], adjT[:, c, :]).then_inc(sem("adjT_r"), 1)

                def split(x, c, done):
                    after(step(dve.tensor_copy(x_hi[:, c, :], x[:, c, :])))
                    dve.tensor_tensor(x_lo[:, c, :], x[:, c, :], x_hi[:, c, :].bitcast(F32),
                                      ALU.subtract).then_inc(sem(done), 1)

                split_weight("lin")
                for c in range(C):
                    if c == C - 1:
                        T_lo("hT2", 0)
                        T_lo("hT2", 1)
                    dve.wait_ge(sem("ff2_psum"), c + 1)
                    dve.wait_ge(sem("h1_plus_b2"), c + 1)
                    after(step(dve.tensor_tensor(hr[:, c, :], bank[c][:, :], vr[:, c, :], ALU.add)))
                    norm_stats(2, hr[:, c, :], c)
                    dve.wait_ge(sem("x_plus"), c + 1)
                    affine_norm(2, hr[:, c, :], c, "g2", xr[:, c, :], xr[:, c, :], "x1")
                    dve.wait_ge(sem("x1"), c + 1)
                    norm_stats(3, xr[:, c, :], c)
                    nbias(3, c)
                need_row(dve, "lin_b")
                need_row(dve, "lin_a")
                for c in range(C):
                    if c < 2:
                        T_lo("hT2", c + 2)
                    dve.wait_ge(sem("lin_psum"), c + 1)
                    after(step(dve.tensor_tensor(s1[:, c, :], bank[c][:, :], row("lin_b"), ALU.add)))
                    after(step(dve.scalar_tensor_tensor(s0[:, c, :], s1[:, c, :], 0.0, row("lin_a"),
                                                        ALU.min, ALU.mult)))
                    after(step(dve.scalar_tensor_tensor(vr[:, c, :], s1[:, c, :], 0.0, s0[:, c, :], ALU.max,
                                                        ALU.add)))
                    split(vr, c, "x2")
                split_weight("c1_0")
                for c in range(C):
                    T_lo("agg0", c)
                split_weight("c2_0")

                def batch_scale(l, c):
                    dve.wait_ge(sem("rstd"), norms(4 + l, c))
                    after(step(dve.tensor_scalar(st(4 + l, c, 10), st(4 + l, c, 9), col("gam", l * C + c), None,
                                                 ALU.mult)))
                    after(step(dve.tensor_scalar(st(4 + l, c, 11), st(4 + l, c, 6), st(4 + l, c, 10), -1.0,
                                                 ALU.mult, ALU.mult)))
                    dve.tensor_scalar(st(4 + l, c, 11), st(4 + l, c, 11), col("bet", l * C + c), None,
                                      ALU.add).then_inc(sem(f"bnb{l}"), 1)

                def x3_lo(c):
                    dve.wait_ge(sem("x3_hi"), c + 1)
                    dve.tensor_tensor(x_lo[:, :, blk(P, c)], bank[4 + c % 2][:, :].rearrange("p (f n) -> p f n", f=C),
                                      x_hi[:, :, blk(P, c)].bitcast(F32), ALU.subtract).then_inc(sem("x3"), 1)

                for l in range(2):
                    for c in range(C):
                        dve.wait_ge(sem(f"c1_{l}_sum"), c + 1)
                        after(step(dve.tensor_scalar(vr[:, c, :], s0[:, c, :], 0.0, alph[:, l:l + 1], ALU.min,
                                                     ALU.mult)))
                        after(step(dve.scalar_tensor_tensor(vr[:, c, :], s0[:, c, :], 0.0, vr[:, c, :], ALU.max,
                                                            ALU.add)))
                        split(vr, c, f"c1_{l}")
                    for c in range(C + 1):
                        if c < C:
                            dve.wait_ge(sem(f"c2_{l}"), c + 1)
                            norm_stats(4 + l, s1[:, c, :], c)
                        if l == 0 and c == C:
                            x3_lo(0)
                        if c:
                            batch_scale(l, c - 1)
                    if l == 0:
                        x3_lo(1)
                        split_weight("c1_1", (0, 1))
                        x3_lo(2)
                        T_lo("agg1", 0)
                        split_weight("c1_1", (2,))
                        x3_lo(3)
                        split_weight("c1_1", (3,))
                        for c in range(1, C):
                            T_lo("agg1", c)
                        split_weight("c2_1")
                for c in range(C + 2):
                    if c < C:
                        dve.wait_ge(sem("x4_psum"), c + 1)
                        dve.tensor_tensor(xr[:, c, :], xr[:, c, :], bank[c][:, :], ALU.add).then_inc(
                            sem("x5"), 1)
                        dve.wait_ge(sem("x5"), c + 1)
                        norm_stats(6, xr[:, c, :], c)
                    if 1 <= c <= C:
                        dve.wait_ge(sem("dinv"), 1)
                        dve.wait_ge(sem("rstd"), norms(6, c - 1))
                        scale, bias = gcn_s[:, c - 1, 3:4], gcn_s[:, c - 1, 4:5]
                        after(step(dve.tensor_scalar(scale, st(6, c - 1, 9), gcn_s[:, c - 1, 2:3], None, ALU.mult)))
                        dve.tensor_scalar(bias, st(6, c - 1, 6), scale, -1.0, ALU.mult, ALU.mult).then_inc(
                            sem("gcn_nb"), 1)
                    if c >= 2:
                        dve.wait_ge(sem("h_gcn_hi"), c - 1)
                        dve.tensor_tensor(x_lo[:, c - 2, :], hr[:, c - 2, :], x_hi[:, c - 2, :].bitcast(F32),
                                          ALU.subtract).then_inc(sem("h_gcn_parts"), 1)
                need_row(dve, "gcn_b")
                split_weight("gcn")
                for c in range(C):
                    T_lo("agg2", c)
                for c in range(C):
                    dve.wait_ge(sem("gcn_psum"), c + 1)
                    after(step(dve.scalar_tensor_tensor(s0[:, c, :], bank[c][:, :], gcn_s[:, c, 2:3], row("gcn_b"),
                                                        ALU.mult, ALU.add)))
                    after(step(dve.scalar_tensor_tensor(s1[:, c, :], s0[:, c, :], 0.01, s0[:, c, :], ALU.mult,
                                                        ALU.max)))
                    dve.wait_ge(sem("h_gcn"), c + 1)
                    dve.tensor_tensor(xr[:, c, :], xr[:, c, :], s1[:, c, :], ALU.add).then_inc(sem("x6"), 1)
                    dve.wait_ge(sem("x6"), c + 1)
                    norm_stats(7, xr[:, c, :], c)
                    if c:
                        nbias(7, c - 1)
                nbias(7, C - 1)
                need_row(dve, "bias1")
                need_row(dve, "bias2")

                def gated_lo(layer, c):
                    for rel, (hi, lo) in enumerate(((gated0_hi, gated0_lo), (gated1_hi, gated1_lo))):
                        dve.wait_ge(sem("gated_hi"), (layer * C + c) * RELS + rel + 1)
                        dve.scalar_tensor_tensor(lo[:, c, :], hr[:, c, :], gate[:, layer, c, rel:rel + 1],
                                                 hi[:, c, :].bitcast(F32), ALU.mult, ALU.subtract).then_inc(
                                                     sem(f"gated{rel}"), 1)

                def G_lo(layer, rel):
                    hi, lo = ((G0_hi, G0_lo), (G1_hi, G1_lo))[rel]
                    for c in range(C):
                        dve.wait_ge(sem("G_hi"), (layer * RELS + rel) * C + c + 1)
                        dve.tensor_tensor(lo[:, c, :], bank[rel * C + c][:, :], hi[:, c, :].bitcast(F32),
                                          ALU.subtract).then_inc(sem(f"G{rel}"), 1)

                def split_w(layer, rel):
                    dve.wait_ge(sem("w_hi"), layer * RELS + rel + 1)
                    dve.tensor_tensor(w_lo[:, blk(C, rel), :], qkw[:, blk(C, rel), :],
                                      w_hi[:, blk(C, rel), :].bitcast(F32), ALU.subtract).then_inc(
                                          sem("w_lo"), 1)

                dve.wait_ge(sem("gcn_psum"), C)
                for rel in range(RELS):
                    dve.tensor_copy(cnt_r[rel][:, :, :], cnt[:, rel, :, :]).then_inc(sem("cnt_r"), 1)
                for c in range(C):
                    gated_lo(0, c)
                split_w(0, 0)
                G_lo(0, 0)
                split_w(0, 1)
                for c in range(C):
                    dve.wait_ge(sem("h_rel0"), c + 1)
                    dve.tensor_tensor(xr[:, c, :], xr[:, c, :], row("bias2"), ALU.add).then_inc(
                        sem("x_plus_bias2"), 1)
                G_lo(0, 1)
                dve.wait_ge(sem("gated0"), C)
                dve.wait_ge(sem("gated1"), C)
                for c in range(C):
                    dve.wait_ge(sem("rel_psum"), c + 1)
                    after(step(dve.tensor_tensor(hr[:, c, :], bank[c][:, :], row("bias1"), ALU.add)))
                    dve.tensor_scalar(hr[:, c, :], hr[:, c, :], 0.0, None, ALU.max).then_inc(sem("rel0_out"), 1)
                    if c:
                        gated_lo(1, c - 1)
                gated_lo(1, C - 1)
                split_w(1, 0)
                G_lo(1, 0)
                split_w(1, 1)
                G_lo(1, 1)
                dve.wait_ge(sem("gated0"), 2 * C)
                dve.wait_ge(sem("gated1"), 2 * C)
                dve.wait_ge(sem("x_plus_bias2"), C)
                for c in range(C):
                    dve.wait_ge(sem("rel_psum"), C + c + 1)
                    dve.tensor_tensor(hr[:, c, :], bank[c][:, :], xr[:, c, :], ALU.add).then_inc(
                        sem("rel1_out_sum"), 1)

            @block.tensor
            def _(pe):
                def turn(src, c, ready, done, free=None):
                    pe.wait_ge(sem(ready), c + 1)
                    if c >= 2:
                        pe.wait_ge(sem(done), c - 1)
                    elif free:
                        pe.wait_ge(sem(free), C)
                    for f in range(C):
                        mm = pe.transpose(bank[4 + c % 2][:, blk(P, f)], src[:, c, blk(P, f)], ident[:, :])
                    mm.then_inc(sem(done + "_psum"), 1)

                unit = iter(range(2 * UNITS))

                def units(n):
                    for u in (next(unit) for _ in range(n)):
                        if u == 0:
                            pe.wait_ge(sem("att_loaded"), 16 * 2 * Q)
                        if u == 1:
                            pe.wait_ge(sem("packed"), 2)
                        if u >= 2:
                            pe.wait_ge(sem("stage_ready"), u - 1)
                        pe.wait_ge(sem(f"basis{u % BATCH}_loaded"), 16 * (u // BATCH + 1))
                        for j in range(COLT):
                            mm = pe.matmul(bank[6 + u % 2][32 * j:32 * j + 32, :], attw[0:KB, u // UNITS, :],
                                           bring[0:KB, u % BATCH, j, :], start=True, stop=True,
                                           tile_position=(0, 32 * j))
                        mm.then_inc(sem("basis_used"), 1)

                IN_PAIRS = [(c, k) for k in range(C) for c in (0, 1)] + [(c, k) for c in (2, 3) for k in range(C)]
                BY_TILE = [(c, k) for c in range(C) for k in range(C)]
                ALL_BANKS = [(c, k) for k in range(C) for c in range(C)]

                def parts_tile(a, b, c, k, t_major):
                    for i, j in ((0, 0), (0, 1), (1, 0)):
                        lhs, rhs = (b[j], a[i]) if t_major else (a[i], b[j])
                        mm = pe.matmul(bank[c][:, :], lhs[:, k, blk(P, c)], rhs[:, k, :],
                                       start=(k == 0 and i == j), stop=(k == C - 1 and i == 1))
                    return mm

                def need_parts(wname):
                    pe.wait_ge(sem("weight_parts"), (IN_PARTS.index(wname) + 1) * C)

                def parts_stage(wname, x, ready, done, order=None, t_major=True):
                    need_parts(wname)
                    seen = 0
                    for c, k in order or IN_PAIRS:
                        need = max(k, c) + 1
                        if ready and need > seen:
                            pe.wait_ge(sem(ready), need)
                            seen = need
                        mm = parts_tile(x, weight_parts(wname), c, k, t_major)
                        if k == C - 1:
                            mm.then_inc(sem(done), 1)

                hT_parts, x_parts = (hT_hi, hT_lo), (x_hi, x_lo)

                def aggregate(ready, done, order=IN_PAIRS, cs=range(C), first_bank=0):
                    def both(dt, counts):
                        seen = 0
                        for c, k in order:
                            if c not in cs:
                                continue
                            need = (k if order is ALL_BANKS else max(k, c)) + 1
                            if ready and need > seen:
                                seen = need
                                pe.wait_ge(sem(ready), seen)
                            for i, x in enumerate((x_hi, x_lo)):
                                mm = pe.matmul(bank[first_bank + c][:, :], x[:, k, blk(P, c)].bitcast(dt), counts[:, k, :],
                                               start=(k == 0 and i == 0), stop=(k == C - 1 and i == 1))
                            if k == C - 1:
                                mm.then_inc(sem(done), 1)

                    with pe.If(fits < 1):
                        both(F32, adjT)
                    with pe.Else():
                        both(F32R, adjT_r)

                def count(n):
                    pe.wait_ge(sem("hot_ready"), 2 * (n + 1) - act_hots(n + 1))
                    if on_act(n):
                        pe.wait_ge(sem("act_hot_ready"), act_hots(n + 1))
                    pe.matmul(bank[7][:, :], hot_d[:, n % HOT, :], hot_s[:, n % HOT, :], start=(n == 0),
                              stop=(n == ECH - 1)).then_inc(sem("hot_used"), 1)

                def qkv_tile(t):
                    which, c = divmod(t, C)
                    w = weight("qkv"[which])
                    if c == 0:
                        need_weight(pe, "qkv"[which])
                    if which:
                        pe.wait_ge(sem("qkv"[which - 1]), c + 1)
                    for k in range(C):
                        a, b = ((w[:, k, blk(P, c)], hT[:, k, :]) if which < 2 else
                                (hT[:, k, blk(P, c)], w[:, k, :]))
                        mm = pe.matmul(bank[c][:, :], a, b, start=(k == 0), stop=(k == C - 1))
                    mm.then_inc(sem("qkv"[which] + "_psum"), 1)

                first, every = FIRST_TILE, TILE_EVERY
                pe.wait_ge(sem("ident"), 1)
                for c in range(C):
                    turn(hr, c, "h0", "hT0")
                for n in range(ECH):
                    count(n)
                    if n == first:
                        pe.wait_ge(sem("hT0"), C)
                    if n >= first and (n - first) % every == 0 and (n - first) // every < 3 * C:
                        qkv_tile((n - first) // every)
                for t in range((ECH - 1 - first) // every + 1, 3 * C):
                    qkv_tile(t)
                pe.wait_ge(sem("ones"), 1)
                units(EARLY_UNITS)
                pe.wait_ge(sem("tally"), 1)
                pe.wait_ge(sem("stage_ready"), EARLY_UNITS)
                pe.matmul(bank[6][0:1, 0:1], tally[:, 3:4], ones[:, :], start=True, stop=True).then_inc(
                    sem("tally_sum"), 1)
                pe.wait_ge(sem("flag"), 1)
                fits = pe.value_load(flag[0:1, 0:1])
                with pe.If(fits < 1):
                    slow_d = s0[:, 0, 0:N // 2].bitcast(BF16)
                    slow_s = s0[:, 1, 0:N // 2].bitcast(BF16)
                    pe.wait_ge(sem("v"), C)
                    pe.wait_ge(sem("zeros"), 1)
                    for r in range(RELS):
                        if r:
                            pe.wait_ge(sem("slow_copied"), C)
                        for c in range(C):
                            mm = pe.matmul(bank[c][:, :], zeros[:, 0:P], zeros[:, :], start=True, stop=False)
                        mm.then_inc(sem("slow_used"), 1)
                        with pe.Fori(0, ECH) as n:
                            pe.wait_ge(sem("slow_hot"), n * 2 + (2 * ECH * r + 2))
                            for c in range(C):
                                mm = pe.matmul(bank[c][:, :], slow_d[:, blk(P, c)], slow_s, start=False, stop=False)
                            mm.then_inc(sem("slow_used"), 1)
                        for c in range(C):
                            mm = pe.matmul(bank[c][:, :], zeros[:, 0:P], zeros[:, :], start=False, stop=True)
                        mm.then_inc(sem("slow_counted"), 1)
                pe.wait_ge(sem("v"), C)
                NH = N // 2
                pe.wait_ge(sem("k"), C)
                pe.wait_ge(sem("cols_loaded"), 32)

                def scores(it):
                    half_n, m = divmod(it, C)
                    for q in range(4):
                        h0 = 4 * (q // 2) + q % 2
                        at = HD * (q % 2)
                        if it or q >= 2:
                            pe.wait_ge(sem("scores"), it * 4 + q - 1)
                        for a in range(2):
                            t = (h0 + 2 * a) // 2
                            mm = pe.matmul(bank[4 + q % 2][:, blk(NH, a)], kT[at:at + HD, t, blk(P, m)],
                                           qT[at:at + HD, t, blk(NH, half_n)], start=True, stop=True)
                        mm.then_inc(sem("scores_psum"), 1)

                scores(0)
                for it in range(2 * C):
                    if it + 1 < 2 * C:
                        scores(it + 1)
                    units(BATCH)
                    half_n, m = divmod(it, C)
                    sc = s01[:, (it % 2) * C:(it % 2 + 1) * C, :].rearrange("p c (a n) -> p (c a) n", a=2)
                    pe.wait_ge(sem("probs"), it + 1)
                    for h in range(HEADS):
                        at = HD * (h % 2)
                        mm = pe.matmul(bank[h // 2][at:at + HD, blk(NH, half_n)], vr[:, m, blk(HD, h)],
                                       sc[:, h, :], start=(m == 0), stop=False, skip_group_check=True)
                    for t in range(C):
                        mm = pe.matmul(bank[t][:, blk(NH, half_n)], vr[:, m, blk(P, t)],
                                       no_edge[:, m, blk(NH, half_n)], start=False, stop=(m == C - 1),
                                       skip_group_check=True)
                    mm.then_inc(sem("pv_used"), 1)
                units(2)
                need_weight(pe, "o")
                for c, k in IN_PAIRS:
                    pe.wait_ge(sem("ao"), max(c, k) + 1)
                    mm = pe.matmul(bank[c][:, :], s0[:, k, blk(P, c)], weight("o")[:, k, :], start=(k == 0),
                                   stop=(k == C - 1))
                    if k == C - 1:
                        mm.then_inc(sem("o_psum"), 1)
                for c in range(C):
                    turn(qT, c, "adj", "adjT")
                units(4)
                for c in range(C):
                    turn(vr, c, "h1", "h1T", "adjT")
                pe.wait_ge(sem("h1T"), C)
                parts_stage("f1a", hT_parts, None, "ff1_psum", order=BY_TILE)
                parts_stage("f1b", hT_parts, "ff1", "ff1_psum", order=BY_TILE)
                units(2)
                need_weight(pe, "f2a")
                need_weight(pe, "f2b")
                w_a, w_b = weight("f2a"), weight("f2b")
                for c in range(C):
                    if c == C - 1:
                        turn(hr, 0, "h2", "hT2", "h1T")
                        turn(hr, 1, "h2", "hT2", "h1T")
                    for k in range(2 * C):
                        pe.wait_ge(sem("ff1"), max(k + 1, C + c + 1))
                        mm = pe.matmul(bank[c][:, :], s01[:, k, blk(P, c)], (w_a if k < C else w_b)[:, k % C, :],
                                       start=(k == 0), stop=(k == 2 * C - 1))
                    mm.then_inc(sem("ff2_psum"), 1)
                need_parts("lin")

                def lin_tile(c):
                    pe.wait_ge(sem("hT2"), c + 1)
                    pe.wait_ge(sem("x1"), c + 1)
                    for k in range(C):
                        mm = parts_tile(hT_parts, weight_parts("lin"), c, k, False)
                    mm.then_inc(sem("lin_psum"), 1)

                lin_tile(0)
                turn(hr, 2, "h2", "hT2")
                lin_tile(1)
                turn(hr, 3, "h2", "hT2")
                lin_tile(2)
                lin_tile(3)
                units(2)
                pe.wait_ge(sem("adjT_r"), C)
                pe.wait_ge(sem("stage_ready"), EARLY_UNITS + 2 * C * BATCH + 10)
                aggregate("x2", "agg0_psum", order=ALL_BANKS, first_bank=C)
                parts_stage("c1_0", hT_parts, "agg0", "c1_0_psum")
                units(2)
                parts_stage("c2_0", x_parts, "c1_0", "c2_0_psum")

                def aggregate_column(c):
                    pe.wait_ge(sem("x3"), c + 1)
                    aggregate(None, "agg1_psum", order=BY_TILE, cs=(c,))

                turn(s1, 0, "bn0", "x3", "hT2")
                turn(s1, 1, "bn0", "x3", "hT2")
                units(2)
                aggregate_column(0)
                turn(s1, 2, "bn0", "x3")
                aggregate_column(1)
                turn(s1, 3, "bn0", "x3")
                aggregate_column(2)
                aggregate_column(3)
                units(2)
                parts_stage("c1_1", hT_parts, "agg1", "c1_1_psum")
                parts_stage("c2_1", x_parts, "c1_1", "c2_1_psum")
                units(2)
                pe.wait_ge(sem("c2_1"), C)
                for f in range(C):
                    pe.wait_ge(sem("bn1"), f + 1)
                    for c in range(C):
                        mm = pe.transpose(bank[c][:, blk(P, f)], s1[:, f, blk(P, c)], ident[:, :])
                        if f == C - 1:
                            mm.then_inc(sem("x4_psum"), 1)
                units(4)
                pe.wait_ge(sem("x5"), C)
                aggregate("h_gcn_parts", "agg2_psum", order=ALL_BANKS)
                units(2)
                parts_stage("gcn", hT_parts, "agg2", "gcn_psum", t_major=False)
                def gates(layer, c):
                    pe.wait_ge(sem(f"relT{layer}"), c + 1)
                    for k in range(C):
                        mm = pe.matmul(bank[4 + c % 2][:, 0:RELS], hT[:, k, blk(P, c)],
                                       col(f"gw{layer + 1}", k * RELS, RELS), start=(k == 0), stop=(k == C - 1))
                    mm.then_inc(sem("gates_psum"), 1)

                def G(layer, rel, ks):
                    parts = ((gated0_hi, gated0_lo), (gated1_hi, gated1_lo))[rel]

                    def rounds(dt, counts):
                        for k in ks:
                            pe.wait_ge(sem(f"gated{rel}"), layer * C + k + 1)
                            for f in range(C):
                                if k == 0 and layer and not rel:
                                    pe.wait_ge(sem("rel0_out"), f + 1)
                                for i, g in enumerate(parts):
                                    mm = pe.matmul(bank[rel * C + f][:, :], g[:, k, blk(P, f)].bitcast(dt),
                                                   counts[:, k, :], start=(k == 0 and i == 0),
                                                   stop=(k == C - 1 and i == 1))
                                if k == C - 1:
                                    mm.then_inc(sem(f"G{rel}_psum"), 1)

                    with pe.If(fits < 1):
                        rounds(F32, cnt[:, rel, :, :])
                    with pe.Else():
                        pe.wait_ge(sem("cnt_r"), RELS)
                        rounds(F32R, cnt_r[rel])

                def rel_tile(layer, c):
                    w = weight(f"root{layer + 1}")
                    pe.wait_ge(sem("G0"), layer * C + c + 1)
                    for k in range(C):
                        pe.matmul(bank[c][:, :], hT[:, k, blk(P, c)], w[:, k, :], start=(k == 0), stop=False)
                    if c == 0:
                        pe.wait_ge(sem("w_lo"), RELS * (layer + 1))
                        pe.wait_ge(sem("G1"), (layer + 1) * C)
                    for rel, (g_hi, g_lo) in enumerate(((G0_hi, G0_lo), (G1_hi, G1_lo))):
                        for k in range(C):
                            for a, b in ((g_hi, w_hi), (g_hi, w_lo), (g_lo, w_hi)):
                                mm = pe.matmul(bank[c][:, :], a[:, k, blk(P, c)], b[:, rel * C + k, :],
                                               start=False, stop=(rel == 1 and k == C - 1 and a is g_lo))
                    mm.then_inc(sem("rel_psum"), 1)

                def turn_rel(layer, ready, c, free):
                    if c >= 2:
                        pe.wait_ge(sem("sigmoid"), layer * C + c - 1)
                    turn(hr, c, ready, f"relT{layer}", free)

                turn_rel(0, "h_rel0", 0, "x5")
                units(2)
                turn_rel(0, "h_rel0", 1, "x5")
                gates(0, 0)
                gates(0, 1)
                units(2)
                turn_rel(0, "h_rel0", 2, None)
                turn_rel(0, "h_rel0", 3, None)
                gates(0, 2)
                gates(0, 3)
                pe.wait_ge(sem("stage_ready"), 2 * UNITS)
                G(0, 0, range(C))
                G(0, 1, range(C))
                need_weight(pe, "root1")
                rel_tile(0, 0)
                rel_tile(0, 1)
                for c in range(C - 1):
                    turn_rel(1, "rel0_out", c, "G1")
                    gates(1, c)
                    if c + 2 < C:
                        rel_tile(0, c + 2)
                G(1, 0, (0,))
                turn_rel(1, "rel0_out", C - 1, None)
                gates(1, C - 1)
                G(1, 0, range(1, C))
                G(1, 1, range(C))
                need_weight(pe, "root2")
                for c in range(C):
                    rel_tile(1, c)


def _chunked(w):
    return np.ascontiguousarray(w.reshape(C, P, -1).transpose(1, 0, 2))


def kernel(**inputs):
    import concourse.bacc as bacc
    from concourse.bass_utils import run_bass_kernel_spmd

    i = {k: np.asarray(v) for k, v in inputs.items()}
    edge = {k: np.ascontiguousarray(i[k].reshape(ECH, P).T) for k in ("src", "dst", "edge_type_2")}
    w1, w2 = i["L0_gnn_W1"], i["L0_gnn_W2"]
    conv1, conv2 = i["L1_gnn_conv_W1"], i["L1_gnn_conv_W2"]
    weights = np.stack([_chunked(w) for w in (
        i["L0_gnn_Wq"], i["L0_gnn_Wk"], i["L0_gnn_Wv"], i["L0_gnn_Wo"], w1[:, :D], w1[:, D:], w2[:D], w2[D:],
        i["L1_gnn_lin_W"].T, conv1[0].T, conv2[0].T, conv1[1].T, conv2[1].T,
        i["L2_gnn_W"], i["L3_gnn_root1"], i["L3_gnn_root2"])])
    rows = np.stack([i[k] for k in (
        "L0_gnn_bv", "L0_gnn_bo", "L0_gnn_g1", "L0_gnn_be1", "L0_gnn_b2", "L0_gnn_g2", "L0_gnn_be2",
        "L1_gnn_lin_b", "L1_gnn_lin_a", "L2_gnn_b", "L3_gnn_bias1", "L3_gnn_bias2")])
    cols = np.concatenate([i[k].reshape(-1, P).T for k in (
        "L0_gnn_bq", "L0_gnn_bk", "L0_gnn_b1", "L1_gnn_conv_b1", "L1_gnn_conv_b2", "L1_gnn_bn_gamma",
        "L1_gnn_bn_beta")] + [
            i[k][:, :, 0].reshape(RELS, C, P).transpose(2, 1, 0).reshape(P, -1)
            for k in ("L3_gnn_gate_w1", "L3_gnn_gate_w2")], axis=1)
    basis = np.concatenate([
        i[k].reshape(BASES, C, COLT, UNITS, D).transpose(3, 1, 0, 2, 4).reshape(UNITS, KB, COLT, D)
        for k in ("L3_gnn_basis1", "L3_gnn_basis2")])
    att = np.stack([i["L3_gnn_att1"], i["L3_gnn_att2"]])
    arrays = {"x": _chunked(i["x"]), "src": edge["src"], "dst": edge["dst"], "etype": edge["edge_type_2"],
              "weights": weights, "rows": rows, "cols": cols, "alphas": i["L1_gnn_conv_a"], "att": att,
              "basis": basis}
    arrays = {k: np.ascontiguousarray(a) for k, a in arrays.items()}

    nc = bacc.Bacc("TRN2", target_bir_lowering=False, num_devices=1)
    args = [nc.dram_tensor(f"in_{k}", a.shape, mybir.dt.from_np(a.dtype), kind="ExternalInput").ap()
            for k, a in arrays.items()]
    scratch = nc.dram_tensor("w_scratch", (2, P, Q, D), F32, kind="Internal").ap()
    out = nc.dram_tensor("out_0", (P, C, D), F32, kind="ExternalOutput").ap()
    build(nc, *args, scratch, out)
    r = run_bass_kernel_spmd(nc, [{f"in_{k}": a for k, a in arrays.items()}], core_ids=[0])
    return np.ascontiguousarray(r.results[0]["out_0"].transpose(1, 0, 2)).reshape(N, D)
```
